# Optimizing a Trainium2 kernel written in Bass

```python
import numpy as np
import jax
import jax.numpy as jnp

def _softmax(x, axis=-1):
    return jax.nn.softmax(x, axis=axis)

def _gelu(x):
    return jax.nn.gelu(x, approximate=True)

def _silu(x):
    return jax.nn.silu(x)

def _sigmoid(x):
    return jax.nn.sigmoid(x)

def _layernorm(x, axis=-1, eps=1e-05):
    m = jnp.mean(x, axis=axis, keepdims=True)
    v = jnp.var(x, axis=axis, keepdims=True)
    return (x - m) / jnp.sqrt(v + eps)

def _scatter_add(tgt, idx, src, axis=0):
    return tgt.at[idx].add(src)

def _segment_sum(src, seg, n):
    return jax.ops.segment_sum(src, seg, n)
kernel_name = 'mk_hybrid_d1_jaxref_r8_677da6'

def setup_inputs(seed: int=0):
    np.random.seed(seed)
    _w = jnp.asarray

    def _L0_attn_a_setup():
        import jax, jax.numpy as jnp
        import numpy as np
        H = 16
        CHUNK = 64
        EPS = 1e-05

        def _forward(x, wq, wk, wv, wo, fq1_w, fq1_b, fq2_w, fq2_b, fk1_w, fk1_b, fk2_w, fk2_b, norm_w):
            B, L, D = x.shape
            dk = D // H

            def proj(w):
                return (x @ w.T).reshape(B, L, H, dk).transpose(0, 2, 1, 3)
            q, k, v = (proj(wq), proj(wk), proj(wv))
            q = (q @ fq1_w.T + fq1_b) * (q @ fq2_w.T + fq2_b)
            k = (k @ fk1_w.T + fk1_b) * (k @ fk2_w.T + fk2_b)
            scale = dk ** (-0.5)
            n = L // CHUNK
            qc = q.reshape(B, H, n, CHUNK, dk) * scale
            kc = k.reshape(B, H, n, CHUNK, dk)
            vc = v.reshape(B, H, n, CHUNK, dk)
            kv = jnp.einsum('bhncd,bhnce->bhnde', kc, vc)
            kv = jnp.cumsum(kv, axis=2)
            kv = jnp.concatenate([jnp.zeros_like(kv[:, :, :1]), kv[:, :, :-1]], axis=2)
            inter = jnp.einsum('bhncd,bhnde->bhnce', qc, kv)
            s = jnp.einsum('bhncd,bhnmd->bhncm', qc, kc)
            mask = jnp.tril(jnp.ones((CHUNK, CHUNK), bool))
            s = jnp.where(mask, s, 0.0)
            intra = jnp.einsum('bhncm,bhnmd->bhncd', s, vc)
            o = (inter + intra).reshape(B, H, L, dk)
            o = o * jax.lax.rsqrt(jnp.mean(o * o, axis=-1, keepdims=True) + EPS) * norm_w
            o = o.transpose(0, 2, 1, 3).reshape(B, L, D)
            return o @ wo.T
        key = jax.random.key(seed)
        ks = jax.random.split(key, 16)
        B, L, D = (2, 512, 256)
        dk = D // H
        g = 2 ** (-2.5)

        def xav(k, n):
            lim = g * np.sqrt(6.0 / (2 * n))
            return jax.random.uniform(k, (n, n), jnp.float32, -lim, lim)
        return {'x': jax.random.normal(ks[0], (B, L, D), jnp.float32), 'wq': xav(ks[1], D), 'wk': xav(ks[2], D), 'wv': xav(ks[3], D), 'wo': xav(ks[4], D), 'fq1_w': xav(ks[5], dk), 'fq1_b': jnp.zeros((dk,), jnp.float32), 'fq2_w': xav(ks[6], dk), 'fq2_b': jnp.zeros((dk,), jnp.float32), 'fk1_w': xav(ks[7], dk), 'fk1_b': jnp.zeros((dk,), jnp.float32), 'fk2_w': xav(ks[8], dk), 'fk2_b': jnp.zeros((dk,), jnp.float32), 'norm_w': jnp.ones((dk,), jnp.float32)}
    _L0_attn_a_in = _L0_attn_a_setup()

    def _L0_attn_b_setup():
        import jax, jax.numpy as jnp
        import numpy as np
        B, T, C, H = (2, 256, 256, 16)
        D = C // H

        def _rope(x):
            t = x.shape[-2]
            d = x.shape[-1]
            freqs = jnp.arange(0, d, 2, dtype=jnp.float32) / d
            angles = jnp.arange(t, dtype=jnp.float32)[:, None] * freqs[None, :]
            emb = jnp.concatenate([jnp.sin(angles), jnp.cos(angles)], axis=-1)
            return x * emb
        key = jax.random.key(seed)
        k0, k1, k2, k3, k4 = jax.random.split(key, 5)
        s = 1.0 / np.sqrt(C)
        x = jax.random.normal(k0, (B, T, C), dtype=jnp.float32)
        qkv_w = jax.random.normal(k1, (3 * C, C), dtype=jnp.float32) * s
        qkv_b = jax.random.normal(k2, (3 * C,), dtype=jnp.float32) * s
        out_w = jax.random.normal(k3, (C, C), dtype=jnp.float32) * s
        out_b = jax.random.normal(k4, (C,), dtype=jnp.float32) * s
        return {'x': x, 'qkv_w': qkv_w, 'qkv_b': qkv_b, 'out_w': out_w, 'out_b': out_b}
    _L0_attn_b_in = _L0_attn_b_setup()

    def _L0_ffn_setup():
        import jax, jax.numpy as jnp
        import numpy as np
        H = 256
        I = 176
        E = 8
        TOP_K = 2
        N_SHARED = 2
        I_SH = I * N_SHARED
        NORM_TOPK = True

        def _moe_forward(hidden_states, gate_w, expert_gate, expert_up, expert_down, shared_gate, shared_up, shared_down):
            bsz, seq_len, hdim = hidden_states.shape
            x = hidden_states.reshape(-1, hdim)
            logits = x @ gate_w.T
            probs = jax.nn.softmax(logits, axis=-1)
            routing_weights, selected = jax.lax.top_k(probs, TOP_K)
            if NORM_TOPK:
                routing_weights = routing_weights / (routing_weights.sum(axis=-1, keepdims=True) + 1e-20)
            combine = jnp.sum(jax.nn.one_hot(selected, E, dtype=routing_weights.dtype) * routing_weights[..., None], axis=1)
            g_sh = x @ shared_gate.T
            u_sh = x @ shared_up.T
            out = jax.nn.silu(g_sh) * u_sh @ shared_down.T
            g = jnp.einsum('nh,eih->nei', x, expert_gate)
            u = jnp.einsum('nh,eih->nei', x, expert_up)
            y = jnp.einsum('nei,ehi->neh', jax.nn.silu(g) * u, expert_down)
            out = out + jnp.einsum('neh,ne->nh', y, combine)
            return out.reshape(bsz, seq_len, hdim)
        key = jax.random.key(seed)
        ks = jax.random.split(key, 8)
        s = 0.02
        return {'hidden_states': jax.random.normal(ks[0], (1, 128, H), dtype=jnp.float32), 'gate_w': jax.random.normal(ks[1], (E, H), dtype=jnp.float32) * s, 'expert_gate': jax.random.normal(ks[2], (E, I, H), dtype=jnp.float32) * s, 'expert_up': jax.random.normal(ks[3], (E, I, H), dtype=jnp.float32) * s, 'expert_down': jax.random.normal(ks[4], (E, H, I), dtype=jnp.float32) * s, 'shared_gate': jax.random.normal(ks[5], (I_SH, H), dtype=jnp.float32) * s, 'shared_up': jax.random.normal(ks[6], (I_SH, H), dtype=jnp.float32) * s, 'shared_down': jax.random.normal(ks[7], (H, I_SH), dtype=jnp.float32) * s}
    _L0_ffn_in = _L0_ffn_setup()
    _d = {'L0_attn_a_x': _L0_attn_a_in['x'], 'L0_attn_a_wq': _L0_attn_a_in['wq'], 'L0_attn_a_wk': _L0_attn_a_in['wk'], 'L0_attn_a_wv': _L0_attn_a_in['wv'], 'L0_attn_a_wo': _L0_attn_a_in['wo'], 'L0_attn_a_fq1_w': _L0_attn_a_in['fq1_w'], 'L0_attn_a_fq1_b': _L0_attn_a_in['fq1_b'], 'L0_attn_a_fq2_w': _L0_attn_a_in['fq2_w'], 'L0_attn_a_fq2_b': _L0_attn_a_in['fq2_b'], 'L0_attn_a_fk1_w': _L0_attn_a_in['fk1_w'], 'L0_attn_a_fk1_b': _L0_attn_a_in['fk1_b'], 'L0_attn_a_fk2_w': _L0_attn_a_in['fk2_w'], 'L0_attn_a_fk2_b': _L0_attn_a_in['fk2_b'], 'L0_attn_a_norm_w': _L0_attn_a_in['norm_w'], 'L0_attn_b_qkv_w': _L0_attn_b_in['qkv_w'], 'L0_attn_b_qkv_b': _L0_attn_b_in['qkv_b'], 'L0_attn_b_out_w': _L0_attn_b_in['out_w'], 'L0_attn_b_out_b': _L0_attn_b_in['out_b'], 'L0_ffn_gate_w': _L0_ffn_in['gate_w'], 'L0_ffn_expert_gate': _L0_ffn_in['expert_gate'], 'L0_ffn_expert_up': _L0_ffn_in['expert_up'], 'L0_ffn_expert_down': _L0_ffn_in['expert_down'], 'L0_ffn_shared_gate': _L0_ffn_in['shared_gate'], 'L0_ffn_shared_up': _L0_ffn_in['shared_up'], 'L0_ffn_shared_down': _L0_ffn_in['shared_down']}
    _x0 = _d['L0_attn_a_x']
    _d['L0_attn_a_x'] = jax.random.normal(jax.random.fold_in(jax.random.key(seed), 1), (4, 512, 256), dtype=_x0.dtype)
    del _x0
    return _d

def reference(L0_attn_a_x, L0_attn_a_wq, L0_attn_a_wk, L0_attn_a_wv, L0_attn_a_wo, L0_attn_a_fq1_w, L0_attn_a_fq1_b, L0_attn_a_fq2_w, L0_attn_a_fq2_b, L0_attn_a_fk1_w, L0_attn_a_fk1_b, L0_attn_a_fk2_w, L0_attn_a_fk2_b, L0_attn_a_norm_w, L0_attn_b_qkv_w, L0_attn_b_qkv_b, L0_attn_b_out_w, L0_attn_b_out_b, L0_ffn_gate_w, L0_ffn_expert_gate, L0_ffn_expert_up, L0_ffn_expert_down, L0_ffn_shared_gate, L0_ffn_shared_up, L0_ffn_shared_down):

    def _L0_attn_a_ref(x, wq, wk, wv, wo, fq1_w, fq1_b, fq2_w, fq2_b, fk1_w, fk1_b, fk2_w, fk2_b, norm_w):
        import jax, jax.numpy as jnp
        import numpy as np
        H = 16
        CHUNK = 64
        EPS = 1e-05

        def _forward(x, wq, wk, wv, wo, fq1_w, fq1_b, fq2_w, fq2_b, fk1_w, fk1_b, fk2_w, fk2_b, norm_w):
            B, L, D = x.shape
            dk = D // H

            def proj(w):
                return (x @ w.T).reshape(B, L, H, dk).transpose(0, 2, 1, 3)
            q, k, v = (proj(wq), proj(wk), proj(wv))
            q = (q @ fq1_w.T + fq1_b) * (q @ fq2_w.T + fq2_b)
            k = (k @ fk1_w.T + fk1_b) * (k @ fk2_w.T + fk2_b)
            scale = dk ** (-0.5)
            n = L // CHUNK
            qc = q.reshape(B, H, n, CHUNK, dk) * scale
            kc = k.reshape(B, H, n, CHUNK, dk)
            vc = v.reshape(B, H, n, CHUNK, dk)
            kv = jnp.einsum('bhncd,bhnce->bhnde', kc, vc)
            kv = jnp.cumsum(kv, axis=2)
            kv = jnp.concatenate([jnp.zeros_like(kv[:, :, :1]), kv[:, :, :-1]], axis=2)
            inter = jnp.einsum('bhncd,bhnde->bhnce', qc, kv)
            s = jnp.einsum('bhncd,bhnmd->bhncm', qc, kc)
            mask = jnp.tril(jnp.ones((CHUNK, CHUNK), bool))
            s = jnp.where(mask, s, 0.0)
            intra = jnp.einsum('bhncm,bhnmd->bhncd', s, vc)
            o = (inter + intra).reshape(B, H, L, dk)
            o = o * jax.lax.rsqrt(jnp.mean(o * o, axis=-1, keepdims=True) + EPS) * norm_w
            o = o.transpose(0, 2, 1, 3).reshape(B, L, D)
            return o @ wo.T
        return _forward(x, wq, wk, wv, wo, fq1_w, fq1_b, fq2_w, fq2_b, fk1_w, fk1_b, fk2_w, fk2_b, norm_w)

    def _L0_attn_b_ref(x, qkv_w, qkv_b, out_w, out_b):
        import jax, jax.numpy as jnp
        import numpy as np
        B, T, C, H = (2, 256, 256, 16)
        D = C // H

        def _rope(x):
            t = x.shape[-2]
            d = x.shape[-1]
            freqs = jnp.arange(0, d, 2, dtype=jnp.float32) / d
            angles = jnp.arange(t, dtype=jnp.float32)[:, None] * freqs[None, :]
            emb = jnp.concatenate([jnp.sin(angles), jnp.cos(angles)], axis=-1)
            return x * emb
        b, t, c = x.shape
        qkv = x @ qkv_w.T + qkv_b
        qkv = qkv.reshape(b, t, 3, H, D)
        q = jnp.transpose(qkv[:, :, 0], (0, 2, 1, 3))
        k = jnp.transpose(qkv[:, :, 1], (0, 2, 1, 3))
        v = jnp.transpose(qkv[:, :, 2], (0, 2, 1, 3))
        q = _rope(q)
        k = _rope(k)
        scores = jnp.einsum('bhqd,bhkd->bhqk', q, k) / np.sqrt(D)
        causal = jnp.tril(jnp.ones((t, t), dtype=bool))
        scores = jnp.where(causal, scores, -jnp.inf)
        attn = jax.nn.softmax(scores, axis=-1)
        out = jnp.einsum('bhqk,bhkd->bqhd', attn, v).reshape(b, t, c)
        return out @ out_w.T + out_b

    def _L0_ffn_ref(hidden_states, gate_w, expert_gate, expert_up, expert_down, shared_gate, shared_up, shared_down):
        import jax, jax.numpy as jnp
        import numpy as np
        H = 256
        I = 176
        E = 8
        TOP_K = 2
        N_SHARED = 2
        I_SH = I * N_SHARED
        NORM_TOPK = True

        def _moe_forward(hidden_states, gate_w, expert_gate, expert_up, expert_down, shared_gate, shared_up, shared_down):
            bsz, seq_len, hdim = hidden_states.shape
            x = hidden_states.reshape(-1, hdim)
            logits = x @ gate_w.T
            probs = jax.nn.softmax(logits, axis=-1)
            routing_weights, selected = jax.lax.top_k(probs, TOP_K)
            if NORM_TOPK:
                routing_weights = routing_weights / (routing_weights.sum(axis=-1, keepdims=True) + 1e-20)
            combine = jnp.sum(jax.nn.one_hot(selected, E, dtype=routing_weights.dtype) * routing_weights[..., None], axis=1)
            g_sh = x @ shared_gate.T
            u_sh = x @ shared_up.T
            out = jax.nn.silu(g_sh) * u_sh @ shared_down.T
            g = jnp.einsum('nh,eih->nei', x, expert_gate)
            u = jnp.einsum('nh,eih->nei', x, expert_up)
            y = jnp.einsum('nei,ehi->neh', jax.nn.silu(g) * u, expert_down)
            out = out + jnp.einsum('neh,ne->nh', y, combine)
            return out.reshape(bsz, seq_len, hdim)
        return _moe_forward(hidden_states, gate_w, expert_gate, expert_up, expert_down, shared_gate, shared_up, shared_down)
    x = L0_attn_a_x
    x = x + _L0_attn_a_ref(_layernorm(x, axis=-1), L0_attn_a_wq, L0_attn_a_wk, L0_attn_a_wv, L0_attn_a_wo, L0_attn_a_fq1_w, L0_attn_a_fq1_b, L0_attn_a_fq2_w, L0_attn_a_fq2_b, L0_attn_a_fk1_w, L0_attn_a_fk1_b, L0_attn_a_fk2_w, L0_attn_a_fk2_b, L0_attn_a_norm_w)
    x = x + _L0_ffn_ref(_layernorm(x, axis=-1), L0_ffn_gate_w, L0_ffn_expert_gate, L0_ffn_expert_up, L0_ffn_expert_down, L0_ffn_shared_gate, L0_ffn_shared_up, L0_ffn_shared_down)
    x = x + _L0_attn_b_ref(_layernorm(x, axis=-1), L0_attn_b_qkv_w, L0_attn_b_qkv_b, L0_attn_b_out_w, L0_attn_b_out_b)
    x = x + _L0_ffn_ref(_layernorm(x, axis=-1), L0_ffn_gate_w, L0_ffn_expert_gate, L0_ffn_expert_up, L0_ffn_expert_down, L0_ffn_shared_gate, L0_ffn_shared_up, L0_ffn_shared_down)
    return x

_drawn_inputs = setup_inputs


def setup_inputs(seed=0):
    import zlib

    import numpy as np

    out = dict(_drawn_inputs(seed))
    spreads = {'L0_attn_a_fq1_b': (0.0, 0.703),
     'L0_attn_a_fq2_b': (0.0, 0.701),
     'L0_attn_a_fk1_b': (0.0, 0.722),
     'L0_attn_a_fk2_b': (0.0, 0.8),
     'L0_attn_a_norm_w': (1.0, 0.6)}
    factors = {'L0_attn_a_wq': 7.776,
     'L0_attn_a_wk': 5.242,
     'L0_attn_a_wv': 4.438,
     'L0_attn_a_wo': 4.46,
     'L0_attn_a_fq1_w': 8.0,
     'L0_attn_a_fq2_w': 8.0,
     'L0_attn_a_fk1_w': 8.0,
     'L0_attn_a_fk2_w': 7.043,
     'L0_ffn_gate_w': 3.448,
     'L0_ffn_expert_gate': 2.993,
     'L0_ffn_expert_up': 2.959,
     'L0_ffn_expert_down': 2.956}
    for name, (base, spread) in spreads.items():
        noise = np.random.default_rng([zlib.crc32(name.encode()), seed]).standard_normal(out[name].shape)
        drawn = base * np.exp(spread * noise) if base else spread * noise
        out[name] = jnp.asarray(drawn.astype(out[name].dtype))
    for name, factor in factors.items():
        out[name] = (out[name] * factor).astype(out[name].dtype)
    return out
```

```python
from contextlib import ExitStack

import numpy as np

import concourse.bass as bass
from concourse import mybir

ALU = mybir.AluOpType
ACT = mybir.ActivationFunctionType
AX_X = mybir.AxisListType.X
F32 = mybir.dt.float32
F32R = mybir.dt.float32r
BF16 = mybir.dt.bfloat16
U32 = mybir.dt.uint32

P = 128
B, L, D = 4, 512, 256
T = L // P
KD = D // P
H = 16
DK = D // H
EPS = 1e-5
E, I, ISH = 8, 176, 352
F = ISH + E * I
FT = -(-F // P)
FP = FT * P
SHARED_TILES = ISH // P
CH = FP // 2
TS = 6
NEG = -1e30

C_ID, C_TRI, C_NEG, C_BD, C_EVEN, C_ODD, C_IOTA, C_HALF, C_EMB, C_END = 0, 128, 256, 384, 512, 513, 514, 522, 538, 1050
V_Q1, V_Q2, V_K1, V_K2, V_NW, V_BQ, V_BK, V_END = 0, 1, 2, 3, 4, 5, 7, 9


def head_of(half, row, odd):
    return half * 8 + 2 * row + odd


def build(nc, x_in, wqk, wv_t, wo_t, fmap, vecs, qkv_t, out_t, rows_b, gate_t, gu_t, down_t, consts, sel_in, out):
    ctx = ExitStack()
    with ctx:
        def sb(name, shape, dt=F32):
            return ctx.enter_context(nc.sbuf_tensor(name, shape, dt))

        def sem(name):
            return ctx.enter_context(nc.semaphore(name))

        w_feat = sb("w_feat", [P, 2, 4, KD, D], F32R)
        w_v = sb("w_v", [P, 2, KD, D], F32R)
        w_o = sb("w_o", [P, 2, KD, D], F32R)
        w_qkv = sb("w_qkv", [P, 2, KD, 3 * D], F32R)
        w_out = sb("w_out", [P, 2, KD, D], F32R)
        w_gate = sb("w_gate", [P, 2, KD, E], F32R)
        w_gu = sb("w_gu", [P, 2, 2, KD, FP], F32R)
        w_dn = sb("w_dn", [P, 2, FT, D], F32R)
        cst = sb("cst", [P, C_END])
        ident = cst[:, C_ID:C_ID + P]
        tri = cst[:, C_TRI:C_TRI + P]
        bdmask = cst[:, C_BD:C_BD + P]
        iota8 = cst[:, C_IOTA:C_IOTA + E]
        emb = cst[:, C_EMB:C_EMB + L]
        ident16 = sb("ident16", [P, P], BF16)
        neg16 = sb("neg16", [P, P], BF16)
        sel16 = sb("sel16", [32, FP], BF16)
        vec = sb("vec", [P, V_END])
        rowb = sb("rowb", [P, 2, D])
        xin = sb("xin", [P, T, D])
        x = sb("x", [P, T, D])
        xn = sb("xn", [P, T, D])
        xt = sb("xt", [P, 2, KD, L], F32R)
        qk = sb("qk", [P, 4, L])
        qs = sb("qs", [P, 2, KD, L], F32R)
        ks = sb("ks", [P, 2, 2, KD, L], F32R)
        hs = ks[:, :, :, :, :].rearrange("p a b c l -> p (a b c) l")
        v = sb("v", [P, T, D])
        work = sb("work", [P, 5, L])
        kvm = sb("kvm", [P, 3, D])
        ktok = xn
        sq = work[:, 4, 0:D]
        wqk_raw = x[:, :, :].rearrange("p (w h) i -> p w h i", w=2)
        bd = work[:, 4, :].rearrange("p (w n) -> p w n", w=4)
        sel_a, sel_b = 1024, FP - 1024
        sel_raw = (xin[0:32, :, :].rearrange("p a l -> p (a l)"), kvm[0:32, :, :].rearrange("p a l -> p (a l)"))
        st6 = sb("st6", [P, T, 6])
        mv = sb("mv", [P, T, 2])
        ve = sb("ve", [P, H])
        rstd = sb("rstd", [P, H])
        ms = sb("ms", [P, H])
        mx = sb("mx", [P, 2, 2])
        nb = sb("nb", [P, 2, 2])
        sums = sb("sums", [P, 2, H])
        rinv = sb("rinv", [P, 2, H])
        ga = sb("ga", [P, T, E])
        gb = sb("gb", [P, T, E])
        gtop = sb("gtop", [P, T, E])
        gidx = sb("gidx", [P, T, E], U32)
        gidf = sb("gidf", [P, T, 2])
        gs = sb("gs", [P, 4, T])
        gw = sb("gw", [P, 2, T])
        geq = sb("geq", [P, 2, T, E])
        cmb = sb("cmb", [P, 3, T, E])
        c16 = sb("c16", [P, T, 32], BF16)
        ct16 = sb("ct16", [32, L], BF16)
        spare = sb("spare", [P, 8])
        fm = sb("fm", [P, 4, DK])
        wflat = work[:, :, :].rearrange("p a l -> p (a l)")
        qflat = qk[:, :, :].rearrange("p a l -> p (a l)")
        xflat = xn[:, :, :].rearrange("p a l -> p (a l)")
        vflat = v[:, :, :].rearrange("p a l -> p (a l)")
        bank = ctx.enter_context(nc.psum_tensor("bank", [P, 8, 512], F32))
        places = [wflat[:, 0:CH], wflat[:, CH:2 * CH], qflat[:, 0:CH], qflat[:, CH:2 * CH], xflat[:, 0:CH], vflat[:, 0:CH]]

        l_cst = sem("l_cst"); l_wa = sem("l_wa"); l_x = sem("l_x")
        pieces = [(wv_t, w_v, None), (wo_t, w_o, V_NW), (out_t, w_out, None), (gate_t, w_gate, None)]
        pieces = [(s.rearrange("(k p) n -> p k n", p=P), w[:, 0], w[:, 1], (KD, s.shape[1]), f) for s, w, f in pieces]
        for k in range(KD):
            pieces.append((qkv_t[k * P:(k + 1) * P, :], w_qkv[:, 0, k, :], w_qkv[:, 1, k, :], (3 * D,), None))
        for g in range(2):
            for k in range(KD):
                for c in range(2):
                    s = slice(c * CH, (c + 1) * CH)
                    pieces.append((gu_t[k * P:(k + 1) * P, g, s], w_gu[:, 0, g, k, s], w_gu[:, 1, g, k, s], (CH,), None))
        for n0 in range(0, FT, 3):
            n1 = min(FT, n0 + 3)
            pieces.append((down_t.rearrange("(n p) o -> p n o", p=P)[:, n0:n1, :], w_dn[:, 0, n0:n1, :],
                           w_dn[:, 1, n0:n1, :], (n1 - n0, D), None))
        NPC, NPL = len(pieces), len(places)

        def staged(i):
            shape = pieces[i][3]
            n = int(np.prod(shape))
            a = places[i % NPL][:, 0:n]
            return a if len(shape) == 1 else a.rearrange("p (a n) -> p a n", a=shape[0])

        l_pc = [sem(f"l_pc{i}") for i in range(NPL)]
        w_hi = sem("w_hi")
        w_lo = sem("w_lo")
        p_bd = sem("p_bd"); p_fold = sem("p_fold"); p_fhi = sem("p_fhi"); p_flo = sem("p_flo"); p_c16 = sem("p_c16")

        s_bn = sem("s_bn"); s_ag = sem("s_ag"); s_ve = sem("s_ve"); s_rs = sem("s_rs")
        s_tok = sem("s_tok")
        s_tr = sem("s_tr")
        s_hi = sem("s_hi")
        s_lo = sem("s_lo")
        s_pj = sem("s_pj")
        s_tmp = sem("s_tmp")
        s_qk = sem("s_qk")
        s_sph = sem("s_sph")
        s_spl = sem("s_spl")
        s_vp = sem("s_vp")
        s_vs = sem("s_vs")
        s_kt = sem("s_kt")
        s_ktok = sem("s_ktok")
        s_kv = sem("s_kv")
        s_kvm = sem("s_kvm")
        s_sc = sem("s_sc")
        s_st = sem("s_st")
        s_pv = sem("s_pv")
        s_sq = sem("s_sq")
        s_ms = sem("s_ms"); s_me = sem("s_me"); s_rr = sem("s_rr")
        s_op = sem("s_op")
        s_res = sem("s_res")
        s_lg = sem("s_lg")
        s_gv = sem("s_gv")
        s_ge = sem("s_ge")
        s_c16 = sem("s_c16")
        s_ctp = sem("s_ctp")
        s_ct = sem("s_ct")
        s_up = sem("s_up")
        s_sg = sem("s_sg")
        s_t1 = sem("s_t1")
        s_h = sem("s_h")
        s_hh = sem("s_hh")
        s_hl = sem("s_hl")
        s_dn = sem("s_dn")
        s_bp = sem("s_bp")
        s_xb = sem("s_xb")
        s_s = sem("s_s")
        s_mx = sem("s_mx"); s_nb = sem("s_nb")
        s_e = sem("s_e")
        s_t = sem("s_t")
        s_pa = sem("s_pa")
        s_pd = sem("s_pd")
        s_pvb = sem("s_pvb")
        s_ri = sem("s_ri")
        s_out = sem("s_out")
        GV = 16
        NS = T * 8

        block = ctx.enter_context(nc.Block())

        @block.sync
        def _(sp):
            sp.dma_start(cst[:, :], consts).then_inc(l_cst, 16)
            sp.dma_start(sel_raw[0], sel_in[:, 0:sel_a]).then_inc(l_cst, 16)
            sp.dma_start(sel_raw[1], sel_in[:, sel_a:FP]).then_inc(l_cst, 16)
            sp.dma_start(wqk_raw, wqk.rearrange("w (h p) i -> p w h i", p=P)).then_inc(l_wa, 16)
            sp.dma_start(fm[:, :, :], fmap).then_inc(l_wa, 16)
            sp.dma_start(vec[:, :], vecs).then_inc(l_wa, 16)
            sp.dma_start(rowb[:, :, :], rows_b).then_inc(s_out, 16)
            for i, (src, _, _, _, _) in enumerate(pieces):
                if i >= NPL:
                    sp.wait_ge(w_lo, i - NPL + 1)
                sp.dma_start(staged(i), src).then_inc(l_pc[i % NPL], 16)
            for b in range(B):
                if b == 0:
                    sp.wait_ge(p_c16, 4)
                else:
                    sp.wait_ge(s_res, 8 * (b - 1) + 2)
                sp.dma_start(xin[:, :, :], x_in[b].rearrange("(t p) d -> p t d", p=P)).then_inc(l_x, 16)
                if b >= 1:
                    sp.wait_ge(s_res, 8 * b)
                    sp.dma_start(out[b - 1].rearrange("(t p) d -> p t d", p=P), x[:, :, :]).then_inc(s_out, 16)
            sp.wait_ge(s_res, 8 * B)
            sp.dma_start(out[B - 1].rearrange("(t p) d -> p t d", p=P), x[:, :, :]).then_inc(s_out, 16)
            sp.wait_ge(s_out, 16 * (B + 1))

        def piece_in(eng, i):
            eng.wait_ge(l_pc[i % NPL], 16 * (i // NPL + 1))

        @block.gpsimd
        def _(pool):
            with pool.Fori(0, B) as b:
                def rsqrt_ln(s):
                    pool.wait_ge(s_ve, b * 4 + (s + 1))
                    nc.gpsimd.tensor_tensor(rstd[:, 0:T], ve[:, 0:T], cst[:, C_HALF:C_HALF + T], ALU.pow).then_inc(s_rs, 1)

                rsqrt_ln(0)
                for c in range(T):
                    pool.wait_ge(s_me, b * T + (c + 1))
                    nc.gpsimd.tensor_tensor(rstd[:, :], ve[:, :], cst[:, C_HALF:C_HALF + H], ALU.pow).then_inc(s_rr, 1)
                rsqrt_ln(1)
                rsqrt_ln(2)
                pool.wait_ge(s_tok, b * (4 * TS) + 16)
                for t in range(T):
                    i = nc.gpsimd.tensor_tensor(x[:, t, :], x[:, t, :], rowb[:, 1, :], ALU.add)
                i.then_inc(s_xb, 1)
                rsqrt_ln(3)

        @block.scalar
        def _(act):
            act.wait_ge(l_wa, 48)
            for w in range(4):
                act.wait_ge(p_fold, w + 1)
                nc.scalar.copy(w_feat[:, 0, w, :, :], bank[:, w, :].rearrange("p (k n) -> p k n", k=KD)).then_inc(p_fhi, 1)
            for i, (_, hi, _, _, factor) in enumerate(pieces):
                piece_in(act, i)
                if factor is None:
                    nc.scalar.copy(hi, staged(i)).then_inc(w_hi, 1)
                else:
                    nc.scalar.activation(hi, staged(i), ACT.Copy, scale=vec[:, factor:factor + 1]).then_inc(w_hi, 1)

            with act.Fori(0, B) as b:
                def split_hi(i):
                    for k in range(KD):
                        act.wait_ge(s_tr, b * (2 * TS) + (2 * i + k + 1))
                        nc.scalar.copy(xt[:, 0, k, :], bank[:, k, :]).then_inc(s_hi, 1)

                def split_qk_hi(stage, n, half, is_q):
                    act.wait_ge(s_qk, b * 8 + (4 * stage + n))
                    if is_q:
                        nc.scalar.copy(qs[:, 0, half, :], qk[:, 2 + half, :]).then_inc(s_sph, 1)
                    else:
                        for odd in range(2):
                            nc.scalar.activation(ks[:, 0, odd, half, :], qk[:, half, :], ACT.Copy,
                                                 scale=cst[:, C_EVEN + odd:C_EVEN + odd + 1]).then_inc(s_sph, 1)

                split_hi(0)
                for j in range(4):
                    act.wait_ge(s_pj, b * 4 + (j + 1))
                    if j >= 2:
                        act.wait_ge(s_qk, b * 8 + (j - 1))
                    nc.scalar.activation(work[:, j % 2, :], bank[:, (2 * j + 2) % 8, :], ACT.Identity,
                                         bias=vec[:, (V_K1, V_K1, V_Q1, V_Q1)[j]:(V_K1, V_K1, V_Q1, V_Q1)[j] + 1]
                                         ).then_inc(s_tmp, 1)
                    if j >= 1:
                        split_qk_hi(0, j, (j - 1) % 2, j - 1 >= 2)
                split_qk_hi(0, 4, 1, True)
                for i in range(2):
                    act.wait_ge(s_vp, b * 4 + (i + 1))
                    nc.scalar.copy(v[:, 2 * i:2 * i + 2, :], bank[:, 2 + i, :].rearrange("p (t n) -> p t n", t=2)
                                   ).then_inc(s_vs, 1)
                for i in range(2):
                    act.wait_ge(s_kt, b * 2 + (i + 1))
                    nc.scalar.copy(ktok[:, :, i * P:(i + 1) * P], bank[:, 4 + i, :].rearrange("p (t n) -> p t n", t=T)
                                   ).then_inc(s_ktok, 1)
                for c in range(T):
                    act.wait_ge(s_pv, b * 8 + 2 * (c + 1))
                    if c:
                        act.wait_ge(s_ms, b * T + c)
                    nc.scalar.activation(sq, bank[:, 6 + c % 2, 0:D], ACT.Square).then_inc(s_sq, 1)
                split_hi(1)

                def ffn(f):
                    split_hi(2 if f == 0 else 5)
                    act.wait_ge(s_gv, b * (2 * GV) + (f * GV + 2))
                    nc.scalar.activation(gb[:, :, :], ga[:, :, :], ACT.Exp).then_inc(s_ge, 1)

                    def high(i):
                        act.wait_ge(s_h, b * (2 * FT) + (f * FT + i + 1))
                        if i >= 3:
                            act.wait_ge(s_dn, b * (2 * FT) + (f * FT + i - 2))
                        nc.scalar.copy(hs[:, 2 * (i % 3), :], work[:, 3 + i % 2, :]).then_inc(s_hh, 1)

                    for i in range(FT):
                        act.wait_ge(s_up, b * (2 * FT) + (f * FT + i + 1))
                        nc.scalar.activation(work[:, i % 2, :], bank[:, 4 + i % 2, :], ACT.Silu).then_inc(s_sg, 1)
                        if i >= 1:
                            high(i - 1)
                    high(FT - 1)

                ffn(0)
                split_hi(3)
                for n in range(4):
                    split_qk_hi(1, n + 1, n % 2, n < 2)

                def exps(p):
                    qt, W = p // 8, (p // 8 + 1) * P
                    for i in range(2):
                        if i == 0:
                            act.wait_ge(s_nb, b * NS + (p + 1))
                            if p >= 2:
                                act.wait_ge(s_t, b * NS + (p - 1))
                        rp, hp = p % 2, p % 8 // 2
                        h = head_of(hp // 2, 2 * rp + i, hp % 2)
                        nc.scalar.activation(work[:, 2 * (p % 2) + i, 0:W], bank[:, 2 * rp + i, 0:W], ACT.Exp,
                                             bias=nb[:, p % 2, i:i + 1], scale=DK ** -0.5,
                                             accum_out=sums[:, qt % 2, h:h + 1]).then_inc(s_e, 1)

                def evac(p):
                    W = (p // 8 + 1) * P
                    act.wait_ge(s_t, b * NS + (p + 1))
                    if p >= 2:
                        act.wait_ge(s_pvb, b * NS + (p - 1))
                    nc.scalar.copy(qk[:, 2 * (p % 2), 0:W], bank[:, 4, 0:W]).then_inc(s_pa, 1)

                for p in range(NS + 1):
                    if p < NS:
                        exps(p)
                    if p >= 1:
                        evac(p - 1)
                split_hi(4)
                ffn(1)

        @block.vector
        def _(dve):
            dve.wait_ge(l_cst, 48)
            nc.vector.tensor_copy(ident16[:, :], ident).then_inc(p_c16, 1)
            nc.vector.tensor_copy(neg16[:, :], cst[:, C_NEG:C_NEG + P]).then_inc(p_c16, 1)
            nc.vector.tensor_copy(sel16[:, 0:sel_a], sel_raw[0]).then_inc(p_c16, 1)
            nc.vector.tensor_copy(sel16[:, sel_a:FP], sel_raw[1]).then_inc(p_c16, 1)
            nc.vector.memset(c16[:, :, 3 * E:32], 0.0).then_inc(p_c16, 1)
            dve.wait_ge(p_c16, 5)
            nc.vector.memset(c16[:, :, 3 * E:3 * E + 1], 1.0).then_inc(p_c16, 1)
            dve.wait_ge(l_wa, 48)
            for w in range(4):
                src = fm[:, w, None, :].broadcast_to([P, P // DK, DK])
                nc.vector.scalar_tensor_tensor(bd[:, w, :].rearrange("p (h d) -> p h d", d=DK), src, DK ** -0.5 if w == 0 else 1.0,
                                               bdmask.rearrange("p (h d) -> p h d", d=DK), ALU.mult, ALU.mult
                                               ).then_inc(p_bd, 1)
            nc.vector.tensor_scalar(vec[:, V_Q1:V_Q1 + 1], vec[:, V_Q1:V_Q1 + 1], DK ** -0.5, None, ALU.mult).then_inc(p_bd, 1)
            for w in range(4):
                dve.wait_ge(p_fhi, w + 1)
                nc.vector.tensor_tensor(w_feat[:, 1, w, :, :], bank[:, w, :].rearrange("p (k n) -> p k n", k=KD),
                                        w_feat[:, 0, w, :, :].bitcast(F32), ALU.subtract).then_inc(p_flo, 1)
            for i, (_, hi, lo, _, factor) in enumerate(pieces):
                dve.wait_ge(w_hi, i + 1)
                if factor is None:
                    nc.vector.tensor_tensor(lo, staged(i), hi.bitcast(F32), ALU.subtract).then_inc(w_lo, 1)
                else:
                    nc.vector.scalar_tensor_tensor(lo, staged(i), vec[:, factor:factor + 1], hi.bitcast(F32),
                                                   ALU.mult, ALU.subtract).then_inc(w_lo, 1)
            dve.wait_ge(w_lo, NPC)

            with dve.Fori(0, B) as b:
                def carry(semaphore, value):
                    dve.wait_ge(semaphore, value)
                    carried[0] += 1
                    nc.vector.tensor_copy(spare[:, carried[0]:carried[0] + 1], cst[:, C_ODD:C_ODD + 1])

                carried = [-1]

                def layernorm(s, i, src):
                    for t in range(T):
                        nc.vector.bn_stats(st6[:, t, :], src[:, t, :]).then_inc(s_bn, 1)
                    carry(s_bn, b * 16 + (4 * s + 4))
                    for t in range(T):
                        nc.vector.bn_aggr(mv[:, t, :], st6[:, t, :]).then_inc(s_ag, 1)
                    dve.wait_ge(s_ag, b * 16 + (4 * s + 4))
                    nc.vector.tensor_scalar(ve[:, 0:T], mv[:, :, 1], EPS, None, ALU.add).then_inc(s_ve, 1)
                    dve.wait_ge(s_rs, b * 4 + (s + 1))
                    for t in range(T):
                        nc.vector.tensor_scalar(xn[:, t, :], src[:, t, :], mv[:, t, 0:1], rstd[:, t:t + 1],
                                                ALU.subtract, ALU.mult).then_inc(s_tok, 1)

                def split_lo(i):
                    for k in range(KD):
                        dve.wait_ge(s_hi, b * (2 * TS) + (2 * i + k + 1))
                        nc.vector.tensor_tensor(xt[:, 1, k, :], bank[:, k, :], xt[:, 0, k, :].bitcast(F32),
                                                ALU.subtract).then_inc(s_lo, 1)

                def split_qk_lo(stage, n, half, is_q):
                    dve.wait_ge(s_sph, b * 12 + (6 * stage + n))
                    if is_q:
                        nc.vector.tensor_tensor(qs[:, 1, half, :], qk[:, 2 + half, :], qs[:, 0, half, :].bitcast(F32),
                                                ALU.subtract).then_inc(s_spl, 1)
                    else:
                        for odd in range(2):
                            nc.vector.scalar_tensor_tensor(ks[:, 1, odd, half, :], qk[:, half, :],
                                                           cst[:, C_EVEN + odd:C_EVEN + odd + 1],
                                                           ks[:, 0, odd, half, :].bitcast(F32),
                                                           ALU.mult, ALU.subtract).then_inc(s_spl, 1)

                def residual(n, first, base):
                    for i in range(2):
                        nc.vector.tensor_tensor(x[:, 2 * i:2 * i + 2, :], base[:, 2 * i:2 * i + 2, :],
                                                bank[:, first + i, :].rearrange("p (t n) -> p t n", t=2),
                                                ALU.add).then_inc(s_res, 1)
                    dve.wait_ge(s_res, b * 8 + (2 * n + 2))

                dve.wait_ge(l_x, b * 16 + 16)
                layernorm(0, 0, xin)
                split_lo(0)
                for j in range(4):
                    dve.wait_ge(s_tmp, b * 4 + (j + 1))
                    v2 = (V_K2, V_K2, V_Q2, V_Q2)[j]
                    nc.vector.scalar_tensor_tensor(qk[:, j, :], bank[:, (2 * j + 3) % 8, :], vec[:, v2:v2 + 1],
                                                   work[:, j % 2, :], ALU.add, ALU.mult).then_inc(s_qk, 1)
                for n, half, is_q in ((2, 0, False), (4, 1, False), (5, 0, True), (6, 1, True)):
                    split_qk_lo(0, n, half, is_q)

                def scores_out(m):
                    dve.wait_ge(s_sc, b * 8 + (m + 1))
                    if m >= 2:
                        dve.wait_ge(s_pv, b * 8 + (m - 1))
                    for i in range(2):
                        nc.vector.tensor_tensor(work[:, 2 * (m % 2) + i, :].rearrange("p (h c) -> p h c", h=4),
                                                bank[:, 2 * (m % 3) + i, :].rearrange("p (h c) -> p h c", h=4),
                                                tri[:, None, :].broadcast_to([P, 4, P]), ALU.mult).then_inc(s_st, 1)

                def states_out():
                    for i, (lo, hi) in enumerate(((0, 2), (2, 3))):
                        dve.wait_ge(s_kv, b * 2 + (i + 1))
                        n = 2 * (hi - lo)
                        nc.vector.tensor_tensor(kvm[:, lo:hi, :].rearrange("p a (h n) -> p (a h) n", n=P),
                                                bank[:, 6 + i, 0:n * P].rearrange("p (a n) -> p a n", n=P),
                                                bdmask[:, None, :].broadcast_to([P, n, P]), ALU.mult).then_inc(s_kvm, 1)

                def norm_1(c):
                    dve.wait_ge(s_sq, b * T + (c + 1))
                    nc.vector.tensor_reduce(ms[:, :], sq.rearrange("p (h d) -> p h d", d=DK), AX_X, ALU.add).then_inc(s_ms, 1)
                    dve.wait_ge(s_ms, b * T + (c + 1))
                    nc.vector.tensor_scalar(ve[:, :], ms[:, :], 1.0 / DK, EPS, ALU.mult, ALU.add).then_inc(s_me, 1)

                def norm_2(c):
                    dve.wait_ge(s_rr, b * T + (c + 1))
                    nc.vector.tensor_tensor(xn[:, c, :].rearrange("p (h d) -> p h d", d=DK),
                                            bank[:, 6 + c % 2, 0:D].rearrange("p (h d) -> p h d", d=DK),
                                            rstd[:, :, None].broadcast_to([P, H, DK]), ALU.mult).then_inc(s_tok, 1)

                scores_out(0)
                states_out()
                scores_out(1)
                scores_out(2)
                scores_out(3)
                norm_1(0)
                scores_out(4)
                norm_2(0)
                scores_out(5)
                norm_1(1)
                scores_out(6)
                norm_2(1)
                scores_out(7)
                norm_1(2)
                norm_2(2)
                norm_1(3)
                norm_2(3)
                split_lo(1)
                dve.wait_ge(s_op, b * 4 + 2)
                dve.wait_ge(s_out, b * 16 + 16)
                residual(0, 2, xin)

                def ffn(f):
                    i0 = 2 if f == 0 else 5
                    layernorm(1 if f == 0 else 3, i0, x)
                    split_lo(i0)
                    g = [f * GV]

                    def step(ins, wait=True):
                        g[0] += 1
                        ins.then_inc(s_gv, 1)
                        if wait:
                            dve.wait_ge(s_gv, b * (2 * GV) + g[0])

                    def wide(a):
                        return a.broadcast_to([P, T, E])

                    dve.wait_ge(s_lg, b * 2 + (f + 1))
                    lg = bank[:, 2, 0:T * E].rearrange("p (t e) -> p t e", e=E)
                    step(nc.vector.tensor_reduce(gs[:, 0, :], lg, AX_X, ALU.max))
                    step(nc.vector.tensor_tensor(ga[:, :, :], lg, wide(gs[:, 0, :, None]), ALU.subtract), False)
                    dve.wait_ge(s_ge, b * 2 + (f + 1))
                    step(nc.vector.tensor_reduce(gs[:, 1, :], gb[:, :, :], AX_X, ALU.add))
                    step(nc.vector.reciprocal(gs[:, 2, :], gs[:, 1, :]))
                    step(nc.vector.tensor_tensor(ga[:, :, :], gb[:, :, :], wide(gs[:, 2, :, None]), ALU.mult), False)
                    carry(s_gv, b * (2 * GV) + g[0])
                    for t in range(T):
                        ins = nc.vector.max(gtop[:, t, :], ga[:, t, :])
                    step(ins, False)
                    carry(s_gv, b * (2 * GV) + g[0])
                    for t in range(T):
                        ins = nc.vector.max_index(gidx[:, t, :], gtop[:, t, :], ga[:, t, :])
                    step(ins)
                    step(nc.vector.tensor_copy(gidf[:, :, :], gidx[:, :, 0:2]), False)
                    step(nc.vector.scalar_tensor_tensor(gs[:, 3, :], gtop[:, :, 0], 1e-20, gtop[:, :, 1], ALU.add, ALU.add))
                    step(nc.vector.reciprocal(gs[:, 1, :], gs[:, 3, :]))
                    for j in range(2):
                        nc.vector.tensor_tensor(gw[:, j, :], gtop[:, :, j], gs[:, 1, :], ALU.mult)
                        ins = nc.vector.tensor_tensor(geq[:, j, :, :], iota8[:, None, :].broadcast_to([P, T, E]),
                                                      wide(gidf[:, :, j:j + 1]), ALU.is_equal)
                    step(ins)
                    for j in range(2):
                        ins = nc.vector.tensor_tensor(cmb[:, j, :, :], geq[:, j, :, :], wide(gw[:, j, :, None]), ALU.mult)
                    step(ins)
                    step(nc.vector.tensor_tensor(ga[:, :, :], cmb[:, 0, :, :], cmb[:, 1, :, :], ALU.add))
                    step(nc.vector.tensor_copy(c16[:, :, 0:E], ga[:, :, :]))
                    step(nc.vector.tensor_tensor(cmb[:, 2, :, :], ga[:, :, :], c16[:, :, 0:E], ALU.subtract))
                    step(nc.vector.tensor_copy(c16[:, :, E:2 * E], cmb[:, 2, :, :]))
                    assert g[0] == f * GV + GV
                    nc.vector.tensor_tensor(c16[:, :, 2 * E:3 * E], cmb[:, 2, :, :], c16[:, :, E:2 * E],
                                            ALU.subtract).then_inc(s_c16, 1)

                    def n(i):
                        return b * (2 * FT) + (f * FT + i + 1)

                    def low(i):
                        dve.wait_ge(s_hh, n(i))
                        nc.vector.tensor_tensor(hs[:, 2 * (i % 3) + 1, :], work[:, 3 + i % 2, :],
                                                hs[:, 2 * (i % 3), :].bitcast(F32), ALU.subtract).then_inc(s_hl, 1)

                    for i in range(FT):
                        if i == SHARED_TILES:
                            dve.wait_ge(s_ctp, b * 2 + (f + 1))
                            nc.vector.tensor_copy(ct16[:, :], bank[0:32, 3, 0:256].bitcast(BF16)).then_inc(s_ct, 1)
                        dve.wait_ge(s_sg, n(i))
                        if i < SHARED_TILES:
                            nc.vector.tensor_tensor(work[:, 3 + i % 2, :], bank[:, 6 + i % 2, :], work[:, i % 2, :],
                                                    ALU.mult).then_inc(s_h, 1)
                        else:
                            if i > SHARED_TILES:
                                dve.wait_ge(s_h, n(i - 1))
                            nc.vector.tensor_tensor(work[:, 2, :], bank[:, 6 + i % 2, :], work[:, i % 2, :],
                                                    ALU.mult).then_inc(s_t1, 1)
                            dve.wait_ge(s_t1, b * (2 * (FT - SHARED_TILES)) + (f * (FT - SHARED_TILES) + i - SHARED_TILES + 1))
                            nc.vector.tensor_tensor(work[:, 3 + i % 2, :], bank[:, 2 + i % 2, :], work[:, 2, :],
                                                    ALU.mult).then_inc(s_h, 1)
                        if i >= 1:
                            low(i - 1)
                    low(FT - 1)
                    dve.wait_ge(s_dn, n(FT - 1))

                ffn(0)
                residual(1, 0, x)

                layernorm(2, 3, x)
                split_lo(3)
                for n in range(4):
                    dve.wait_ge(s_bp, b * 4 + (n + 1))
                    c = V_BQ + n
                    nc.vector.scalar_tensor_tensor(qk[:, (2 + n) % 4, :], bank[:, 2 + n, :], vec[:, c:c + 1], emb,
                                                   ALU.add, ALU.mult).then_inc(s_qk, 1)
                for i in range(2):
                    dve.wait_ge(s_vp, b * 4 + (2 + i + 1))
                    nc.vector.tensor_tensor(v[:, 2 * i:2 * i + 2, :], bank[:, 6 + i, :].rearrange("p (t n) -> p t n", t=2),
                                            rowb[:, 0, None, :].broadcast_to([P, 2, D]), ALU.add).then_inc(s_vs, 1)
                for n, half, is_q in ((1, 0, True), (2, 1, True), (4, 0, False), (6, 1, False)):
                    split_qk_lo(1, n, half, is_q)

                def maxima(p):
                    W = (p // 8 + 1) * P
                    r = 2 * (p % 2)
                    dve.wait_ge(s_s, b * NS + (p + 1))
                    if p >= 2:
                        dve.wait_ge(s_e, b * (2 * NS) + (2 * p - 2))
                    nc.vector.tensor_reduce(mx[:, p % 2, :], bank[:, r:r + 2, 0:W], AX_X, ALU.max).then_inc(s_mx, 1)
                    dve.wait_ge(s_mx, b * NS + (p + 1))
                    nc.vector.tensor_scalar(nb[:, p % 2, :], mx[:, p % 2, :], -(DK ** -0.5), None, ALU.mult).then_inc(s_nb, 1)

                def evac(p):
                    W = (p // 8 + 1) * P
                    dve.wait_ge(s_t, b * NS + (p + 1))
                    if p >= 2:
                        dve.wait_ge(s_pvb, b * NS + (p - 1))
                    nc.vector.tensor_copy(qk[:, 2 * (p % 2) + 1, 0:W], bank[:, 5, 0:W]).then_inc(s_pd, 1)

                def normalize(qt):
                    dve.wait_ge(s_pvb, b * NS + 8 * (qt + 1))
                    dve.wait_ge(s_e, b * (2 * NS) + 16 * (qt + 1))
                    nc.vector.reciprocal(rinv[:, qt % 2, :], sums[:, qt % 2, :]).then_inc(s_ri, 1)
                    dve.wait_ge(s_ri, b * T + (qt + 1))
                    nc.vector.tensor_tensor(xn[:, qt, :].rearrange("p (h d) -> p h d", d=DK),
                                            bank[:, 6 + qt % 2, 0:D].rearrange("p (h d) -> p h d", d=DK),
                                            rinv[:, qt % 2, :, None].broadcast_to([P, H, DK]), ALU.mult).then_inc(s_tok, 1)

                for p in range(NS + 2):
                    if p < NS:
                        maxima(p)
                    if 1 <= p <= NS:
                        evac(p - 1)
                    if p >= 2 and (p - 2) % 8 == 7:
                        normalize((p - 2) // 8)
                split_lo(4)
                dve.wait_ge(s_op, b * 4 + 4)
                dve.wait_ge(s_xb, b + 1)
                residual(2, 2, x)
                ffn(1)
                residual(3, 0, x)

        @block.tensor
        def _(pe):
            pe.wait_ge(l_cst, 48)
            for w in range(4):
                pe.wait_ge(p_bd, w + 1)
                for k in range(KD):
                    for half in range(KD):
                        ins = nc.tensor.matmul(bank[:, w, (2 * k + half) * P:(2 * k + half + 1) * P],
                                               wqk_raw[:, w // 2, half, k * P:(k + 1) * P], bd[:, w, :],
                                               start=True, stop=True)
                ins.then_inc(p_fold, 1)
            pe.wait_ge(p_flo, 4)
            pe.wait_ge(w_lo, NPC)
            pe.wait_ge(p_c16, 6)

            with pe.Fori(0, B) as b:
                PASSES = ((0, 0), (1, 0), (0, 1))

                def transposed(i):
                    for t in range(T):
                        pe.wait_ge(s_tok, b * (4 * TS) + (4 * i + t + 1))
                        for k in range(KD):
                            ins = nc.tensor.matmul(bank[:, k, t * P:(t + 1) * P], xn[:, t, k * P:(k + 1) * P], ident,
                                                   start=True, stop=True, is_transpose=True)
                            if t == T - 1:
                                ins.then_inc(s_tr, 1)

                def ready(i):
                    pe.wait_ge(s_lo, b * (2 * TS) + (2 * i + 2))

                def by_feature(dst, weight):
                    for n, (k, (a, c)) in enumerate((k, ac) for k in range(KD) for ac in PASSES):
                        ins = nc.tensor.matmul(dst, weight(a, k), xt[:, c, k, :], start=(n == 0), stop=(n == 3 * KD - 1))
                    return ins

                def by_token(dst, t, weight, first):
                    for n, (k, (a, c)) in enumerate((k, ac) for k in range(KD) for ac in PASSES):
                        ins = nc.tensor.matmul(dst, xt[:, a, k, t * P:(t + 1) * P], weight(c, k),
                                               start=(first and n == 0), stop=(n == 3 * KD - 1), skip_group_check=True)
                    return ins

                def two_banks(first, weight, done):
                    for t in range(T):
                        ins = by_token(bank[:, first + t // 2, (t % 2) * D:(t % 2 + 1) * D], t, weight, t % 2 == 0)
                        if t % 2:
                            ins.then_inc(done, 1)

                transposed(0)
                ready(0)
                for j in range(4):
                    half, pair = j % 2, (2, 2, 0, 0)[j]
                    for i in range(2):
                        ins = by_feature(bank[:, (2 * j + 2 + i) % 8, :],
                                         lambda a, k: w_feat[:, a, pair + i, k, half * P:(half + 1) * P])
                    ins.then_inc(s_pj, 1)
                pe.wait_ge(s_qk, b * 8 + 1)
                two_banks(2, lambda c, k: w_v[:, c, k, :], s_vp)
                for half in range(KD):
                    pe.wait_ge(s_qk, b * 8 + 2)
                    for t in range(T):
                        ins = nc.tensor.matmul(bank[:, 4 + half, t * P:(t + 1) * P], qk[:, half, t * P:(t + 1) * P],
                                               ident, start=True, stop=True, is_transpose=True)
                    ins.then_inc(s_kt, 1)

                def scores(m):
                    c = m // 2
                    if m >= 3:
                        pe.wait_ge(s_st, b * 16 + 2 * (m - 2))
                    cols = slice(c * P, (c + 1) * P)
                    for hp in range(4):
                        half, odd = hp // 2, hp % 2
                        for n, (a, q) in enumerate(PASSES):
                            for i in range(2):
                                rows = slice(32 * (2 * (m % 2) + i), 32 * (2 * (m % 2) + i) + 32)
                                ins = nc.tensor.matmul(bank[:, 2 * (m % 3) + i, hp * P:(hp + 1) * P],
                                                       ks[rows, a, odd, half, cols], qs[rows, q, half, cols],
                                                       start=(n == 0), stop=(n == 2))
                    ins.then_inc(s_sc, 1)

                def states():
                    pe.wait_ge(s_ktok, b * 2 + 2)
                    pe.wait_ge(s_vs, b * 4 + 2)
                    for n in range(1, T):
                        for half in range(KD):
                            cols = slice(half * P, (half + 1) * P)
                            at = ((n - 1) % 2) * D + half * P
                            for c in range(n):
                                ins = nc.tensor.matmul(bank[:, 6 + (n - 1) // 2, at:at + P], ktok[:, c, cols],
                                                       v[:, c, cols], start=(c == 0), stop=(c == n - 1))
                        if n >= 2:
                            ins.then_inc(s_kv, 1)

                def products(m):
                    c, o = m // 2, 6 + m // 2 % 2
                    if m % 2 == 0:
                        if c < 2:
                            pe.wait_ge(s_kvm, b * 2 + 2)
                        else:
                            pe.wait_ge(s_tok, b * (4 * TS) + (4 + c - 1))
                        if c:
                            for half in range(KD):
                                cols = slice(half * P, (half + 1) * P)
                                nc.tensor.matmul(bank[:, o, cols], qk[:, 2 + half, c * P:(c + 1) * P],
                                                 kvm[:, c - 1, cols], start=(half == 0), stop=False, skip_group_check=True)
                    pe.wait_ge(s_st, b * 16 + 2 * (m + 1))
                    for hp in range(4):
                        for i in range(2):
                            h = head_of(hp // 2, 2 * (m % 2) + i, hp % 2)
                            ins = nc.tensor.matmul(bank[:, o, h * DK:(h + 1) * DK],
                                                   work[:, 2 * (m % 2) + i, hp * P:(hp + 1) * P],
                                                   v[:, c, h * DK:(h + 1) * DK],
                                                   start=(c == 0 and m % 2 == 0 and hp == 0 and i == 0), stop=True,
                                                   skip_group_check=True)
                    return ins

                pe.wait_ge(s_qk, b * 8 + 4)
                pe.wait_ge(s_spl, b * 12 + 6)
                scores(0)
                states()
                scores(1)
                scores(2)
                for m in range(8):
                    ins = products(m)
                    ins.then_inc(s_pv, 1)
                    if m + 3 < 8:
                        scores(m + 3)
                transposed(1)
                ready(1)
                two_banks(2, lambda c, k: w_o[:, c, k, :], s_op)

                def ffn(f):
                    i0 = 2 if f == 0 else 5
                    transposed(i0)
                    ready(i0)
                    for t in range(T):
                        ins = by_token(bank[:, 2, t * E:(t + 1) * E], t, lambda c, k: w_gate[:, c, k, :], t == 0)
                    ins.then_inc(s_lg, 1)

                    def n(i):
                        return b * (2 * FT) + (f * FT + i + 1)

                    def up(i):
                        cols = slice(i * P, (i + 1) * P)
                        if i >= 2:
                            pe.wait_ge(s_h, n(i - 2))
                        for g in range(2):
                            ins = by_feature(bank[:, 4 + 2 * g + i % 2, :], lambda a, k: w_gu[:, a, g, k, cols])
                        if i == SHARED_TILES:
                            pe.wait_ge(s_c16, b * 2 + (f + 1))
                            for t in range(T):
                                ins = nc.tensor.matmul(bank[0:32, 3, t * 64:(t + 1) * 64].bitcast(BF16), c16[:, t, :],
                                                       ident16[:, :], start=True, stop=True, is_transpose=True)
                            ins.then_inc(s_ctp, 1)
                            pe.wait_ge(s_ct, b * 2 + (f + 1))
                        if i >= SHARED_TILES:
                            ins = nc.tensor.matmul(bank[:, 2 + i % 2, :], sel16[:, cols], ct16[:, :], start=True, stop=True)
                        ins.then_inc(s_up, 1)

                    def down(i):
                        pe.wait_ge(s_hl, n(i))
                        s = 2 * (i % 3)
                        for t in range(T):
                            for a, c in PASSES:
                                ins = nc.tensor.matmul(bank[:, t // 2, (t % 2) * D:(t % 2 + 1) * D],
                                                       hs[:, s + a, t * P:(t + 1) * P], w_dn[:, c, i, :],
                                                       start=(i == 0 and t % 2 == 0 and a == 0 and c == 0),
                                                       stop=(i == FT - 1), skip_group_check=True)
                        ins.then_inc(s_dn, 1)

                    for i in range(FT + 2):
                        if i < FT:
                            up(i)
                        if i >= 2:
                            down(i - 2)

                ffn(0)

                transposed(3)
                ready(3)
                for n in range(4):
                    ins = by_feature(bank[:, 2 + n, :], lambda a, k: w_qkv[:, a, k, n * P:(n + 1) * P])
                    ins.then_inc(s_bp, 1)
                two_banks(6, lambda c, k: w_qkv[:, c, k, 2 * D:3 * D], s_vp)
                pe.wait_ge(s_vs, b * 4 + 4)
                pe.wait_ge(s_qk, b * 8 + 8)
                pe.wait_ge(s_spl, b * 12 + 12)

                def scores_b(p):
                    qt, rp, hp = p // 8, p % 2, p % 8 // 2
                    W, half, odd = (qt + 1) * P, hp // 2, hp % 2
                    if p >= 2:
                        pe.wait_ge(s_e, b * (2 * NS) + (2 * p - 2))
                    for i in range(2):
                        nc.tensor.matmul(bank[:, 2 * rp + i, qt * P:W], ident16[:, :], neg16[:, :],
                                         start=True, stop=False, skip_group_check=True)
                    for n, (a, c) in enumerate(PASSES):
                        for i in range(2):
                            rows = slice(32 * (2 * rp + i), 32 * (2 * rp + i) + 32)
                            ins = nc.tensor.matmul(bank[:, 2 * rp + i, 0:W], qs[rows, a, half, qt * P:W],
                                                   ks[rows, c, odd, half, 0:W], start=False, stop=(n == 2),
                                                   skip_group_check=True)
                    ins.then_inc(s_s, 1)

                def turn(p):
                    qt = p // 8
                    pe.wait_ge(s_e, b * (2 * NS) + (2 * p + 2))
                    if p >= 1:
                        pe.wait_ge(s_pa, b * NS + p)
                        pe.wait_ge(s_pd, b * NS + p)
                    for i in range(2):
                        for kb in range(qt + 1):
                            ins = nc.tensor.matmul(bank[:, 4 + i, kb * P:(kb + 1) * P],
                                                   work[:, 2 * (p % 2) + i, kb * P:(kb + 1) * P], ident,
                                                   start=True, stop=True, is_transpose=True)
                    ins.then_inc(s_t, 1)

                def products_b(p):
                    qt, rp, hp = p // 8, p % 2, p % 8 // 2
                    pe.wait_ge(s_pa, b * NS + (p + 1))
                    pe.wait_ge(s_pd, b * NS + (p + 1))
                    if p % 8 == 0 and qt >= 2:
                        pe.wait_ge(s_tok, b * (4 * TS) + (16 + qt - 1))
                    for i in range(2):
                        h = head_of(hp // 2, 2 * rp + i, hp % 2)
                        for kb in range(qt + 1):
                            ins = nc.tensor.matmul(bank[:, 6 + qt % 2, h * DK:(h + 1) * DK],
                                                   qk[:, 2 * (p % 2) + i, kb * P:(kb + 1) * P],
                                                   v[:, kb, h * DK:(h + 1) * DK], start=(kb == 0), stop=(kb == qt))
                    ins.then_inc(s_pvb, 1)

                for p in range(NS + 2):
                    if p < NS:
                        scores_b(p)
                    if 1 <= p <= NS:
                        turn(p - 1)
                    if p >= 2:
                        products_b(p - 2)
                transposed(4)
                ready(4)
                two_banks(2, lambda c, k: w_out[:, c, k, :], s_op)
                ffn(1)


def _layout(n):
    def tiled(a):
        return np.tile(a, P // DK)

    pad = np.zeros((FP - F, D), np.float32)
    wide = {k: np.asarray(a) for k, a in n.items()}
    gate = np.concatenate([wide["L0_ffn_shared_gate"], wide["L0_ffn_expert_gate"].reshape(E * I, D), pad])
    up = np.concatenate([wide["L0_ffn_shared_up"], wide["L0_ffn_expert_up"].reshape(E * I, D), pad])
    down = np.concatenate([wide["L0_ffn_shared_down"].T,
                           wide["L0_ffn_expert_down"].transpose(0, 2, 1).reshape(E * I, D), pad])
    qkv_b = wide["L0_attn_b_qkv_b"]
    maps = [wide[f"L0_attn_a_{k}_w"] for k in ("fq1", "fq2", "fk1", "fk2")]
    vecs = [tiled(wide[f"L0_attn_a_{k}"]) for k in ("fq1_b", "fq2_b", "fk1_b", "fk2_b", "norm_w")]
    vecs += [qkv_b[i * P:(i + 1) * P] for i in range(4)]
    rows = np.stack([qkv_b[2 * D:3 * D], wide["L0_attn_b_out_b"]])
    return {
        "x": wide["L0_attn_a_x"],
        "wqk": np.stack([wide["L0_attn_a_wq"], wide["L0_attn_a_wk"]]),
        "wv_t": wide["L0_attn_a_wv"].T,
        "wo_t": wide["L0_attn_a_wo"].T,
        "fmap": np.stack([np.tile(m.T, (P // DK, 1)) for m in maps], axis=1),
        "vecs": np.stack(vecs, axis=1),
        "qkv_t": wide["L0_attn_b_qkv_w"].T,
        "out_t": wide["L0_attn_b_out_w"].T,
        "rows_b": np.broadcast_to(rows, (P, 2, D)),
        "gate_t": wide["L0_ffn_gate_w"].T,
        "gu_t": np.stack([gate.T, up.T], axis=1),
        "down_t": down,
        "consts": _constants(),
        "sel": _selector(),
    }


def _constants():
    r = np.arange(P)
    c = np.zeros((P, C_END), np.float32)
    c[:, C_ID:C_ID + P] = r[:, None] == r[None, :]
    c[:, C_TRI:C_TRI + P] = r[:, None] <= r[None, :]
    c[:, C_NEG:C_NEG + P] = np.where(r[None, :] > r[:, None], NEG, 0.0)
    c[:, C_BD:C_BD + P] = r[:, None] // DK == r[None, :] // DK
    c[:, C_EVEN] = r // DK % 2 == 0
    c[:, C_ODD] = r // DK % 2 == 1
    c[:, C_IOTA:C_IOTA + E] = np.arange(E)
    c[:, C_HALF:C_HALF + H] = -0.5
    freqs = np.arange(0, DK, 2, dtype=np.float32) / np.float32(DK)
    angles = np.arange(L, dtype=np.float32)[:, None] * freqs[None, :]
    emb = np.concatenate([np.sin(angles), np.cos(angles)], axis=-1)
    c[:, C_EMB:C_EMB + L] = np.tile(emb.T, (P // DK, 1))
    return c


def _selector():
    s = np.zeros((32, FP), np.float32)
    for j in range(FP):
        if ISH <= j < F:
            for part in range(3):
                s[part * E + (j - ISH) // I, j] = 1.0
        else:
            s[3 * E, j] = 1.0
    return s


def kernel(**inputs):
    import concourse.bacc as bacc
    from concourse.bass_utils import run_bass_kernel_spmd

    nc = bacc.Bacc("TRN2", target_bir_lowering=False, num_devices=1)
    arrays, args = {}, []
    for name, a in _layout(inputs).items():
        a = np.ascontiguousarray(a)
        arrays[f"in_{name}"] = a
        args.append(nc.dram_tensor(f"in_{name}", a.shape, mybir.dt.from_np(a.dtype), kind="ExternalInput").ap())
    args.append(nc.dram_tensor("out_0", (B, L, D), F32, kind="ExternalOutput").ap())
    build(nc, *args)
    r = run_bass_kernel_spmd(nc, [arrays], core_ids=[0])
    return r.results[0]["out_0"]
```

```python
from contextlib import ExitStack

import numpy as np

import concourse.bass as bass
from concourse import mybir

ALU = mybir.AluOpType
ACT = mybir.ActivationFunctionType
AX_X = mybir.AxisListType.X
F32 = mybir.dt.float32
F32R = mybir.dt.float32r
BF16 = mybir.dt.bfloat16
U32 = mybir.dt.uint32

P = 128
B, L, D = 4, 512, 256
T = L // P
KD = D // P
H = 16
DK = D // H
EPS = 1e-5
E, I, ISH = 8, 176, 352
F = ISH + E * I
FT = -(-F // P)
FP = FT * P
SHARED_TILES = ISH // P
CH = FP // 2
TS = 4
NEG = -1e30

C_ID, C_TRI, C_BD, C_EVEN, C_ODD, C_IOTA, C_HALF, C_EMB, C_END = 0, 128, 256, 384, 385, 386, 394, 410, 922
V_Q1, V_Q2, V_K1, V_K2, V_NW, V_BQ, V_BK, V_END = 0, 1, 2, 3, 4, 5, 7, 9


def head_of(half, row, odd):
    return half * 8 + 2 * row + odd


def build(nc, x_in, wqk, wv_t, wo_t, fmap, vecs, qkv_t, out_t, rows_b, gate_t, gu_t, down_t, consts, sel_in, out):
    ctx = ExitStack()
    with ctx:
        def sb(name, shape, dt=F32):
            return ctx.enter_context(nc.sbuf_tensor(name, shape, dt))

        def sem(name):
            return ctx.enter_context(nc.semaphore(name))

        w_feat = sb("w_feat", [P, 2, 4, KD, D], F32R)
        w_v = sb("w_v", [P, 2, KD, D], F32R)
        w_o = sb("w_o", [P, 2, KD, D], F32R)
        w_qkv = sb("w_qkv", [P, 2, KD, 3 * D], F32R)
        w_out = sb("w_out", [P, 2, KD, D], F32R)
        w_gate = sb("w_gate", [P, 2, KD, E], F32R)
        w_gu = sb("w_gu", [P, 2, 2, KD, FP], F32R)
        w_dn = sb("w_dn", [P, 2, FT, D], F32R)
        cst = sb("cst", [P, C_END])
        ident = cst[:, C_ID:C_ID + P]
        tri = cst[:, C_TRI:C_TRI + P]
        bdmask = cst[:, C_BD:C_BD + P]
        iota8 = cst[:, C_IOTA:C_IOTA + E]
        emb = cst[:, C_EMB:C_EMB + L]
        ident16 = sb("ident16", [P, P], BF16)
        neg16 = sb("neg16", [P, P], BF16)
        sel16 = sb("sel16", [32, FP], BF16)
        vec = sb("vec", [P, V_END])
        rowb = sb("rowb", [P, 2, D])
        xin = sb("xin", [P, T, D])
        x = sb("x", [P, T, D])
        xn = sb("xn", [P, T, D])
        xt = sb("xt", [P, 2, KD, L], F32R)
        qk = sb("qk", [P, 4, L])
        ks = sb("ks", [P, 2, KD, L], F32R)
        qs = sb("qs", [P, 2, KD, 2, L], F32R)
        hs = qs[:, :, :, :, :].rearrange("p a b c l -> p (a b c) l")
        vp = sb("vp", [P, T, H // 2, 4, DK])
        work = sb("work", [P, 5, L])
        kvm = sb("kvm", [P, 3, D])
        ktok = xn
        sq = work[:, 4, 0:D]
        scale = work[:, 4, D:2 * D]
        on = xn[:, :, :].rearrange("p a l -> p (a l)").rearrange("p (k l) -> p k l", k=KD)
        wqk_raw = x[:, :, :].rearrange("p (w h) i -> p w h i", w=2)
        bd = work[:, 4, :].rearrange("p (w n) -> p w n", w=4)
        sel_a, sel_b = 1024, FP - 1024
        sel_raw = (xin[0:32, :, :].rearrange("p a l -> p (a l)"), kvm[0:32, :, :].rearrange("p a l -> p (a l)"))
        st6 = sb("st6", [P, T, 6])
        mv = sb("mv", [P, T, 2])
        ve = sb("ve", [P, H])
        rstd = sb("rstd", [P, T])
        sc16 = sb("sc16", [P, 2, H])
        mx = sb("mx", [P, 2, 2])
        nb = sb("nb", [P, 2, 2])
        sums = sb("sums", [P, 2, H])
        kflat = kvm[:, :, :].rearrange("p a n -> p (a n)")

        def small(slot, n, dt=F32):
            a = kflat[:, slot * T * E:(slot + n) * T * E].bitcast(dt)
            return a.rearrange("p (t e) -> p t e", t=T) if n == 1 else a.rearrange("p (n t e) -> p n t e", n=n, t=T)

        ga, gb, gtop, gidx, geq, cmb = small(0, 1), small(1, 1), small(2, 1), small(3, 1, U32), small(4, 2), small(6, 3)
        gidf = sb("gidf", [P, T, 2])
        gs = sb("gs", [P, 4, T])
        gw = sb("gw", [P, 2, T])
        c16 = sb("c16", [P, T, 32], BF16)
        ct16 = kflat[0:32, 12 * T * E:12 * T * E + L // 2].bitcast(BF16)
        spare = sb("spare", [P, 8])
        fm = vp[:, 0, 0, :, :]
        wflat = work[:, :, :].rearrange("p a l -> p (a l)")
        qflat = qk[:, :, :].rearrange("p a l -> p (a l)")
        xflat = xn[:, :, :].rearrange("p a l -> p (a l)")
        bank = ctx.enter_context(nc.psum_tensor("bank", [P, 8, 512], F32))
        places = [wflat[:, 0:CH], wflat[:, CH:2 * CH], qflat[:, 0:CH], qflat[:, CH:2 * CH], xflat[:, 0:CH]]

        l_cst = sem("l_cst"); l_wa = sem("l_wa"); l_x = sem("l_x")
        pieces = [(wv_t, w_v, None), (wo_t, w_o, V_NW), (out_t, w_out, None), (gate_t, w_gate, None)]
        pieces = [(s.rearrange("(k p) n -> p k n", p=P), w[:, 0], w[:, 1], (KD, s.shape[1]), f) for s, w, f in pieces]
        for k in range(KD):
            pieces.append((qkv_t[k * P:(k + 1) * P, :], w_qkv[:, 0, k, :], w_qkv[:, 1, k, :], (3 * D,), None))
        for g in range(2):
            for k in range(KD):
                for c in range(2):
                    s = slice(c * CH, (c + 1) * CH)
                    pieces.append((gu_t[k * P:(k + 1) * P, g, s], w_gu[:, 0, g, k, s], w_gu[:, 1, g, k, s], (CH,), None))
        for n0 in range(0, FT, 3):
            n1 = min(FT, n0 + 3)
            pieces.append((down_t.rearrange("(n p) o -> p n o", p=P)[:, n0:n1, :], w_dn[:, 0, n0:n1, :],
                           w_dn[:, 1, n0:n1, :], (n1 - n0, D), None))
        NPC, NPL = len(pieces), len(places)

        def wide_at(stage, c):
            return x[:, c % 2, :] if stage == 0 else sq

        def v_at(t, h0, h1):
            return vp[:, t, h0 // 2:h1 // 2, 0:4:3, :]

        def staged(i):
            shape = pieces[i][3]
            n = int(np.prod(shape))
            a = places[i % NPL][:, 0:n]
            return a if len(shape) == 1 else a.rearrange("p (a n) -> p a n", a=shape[0])

        l_pc = [sem(f"l_pc{i}") for i in range(NPL)]
        w_hi = sem("w_hi")
        w_lo = sem("w_lo")
        p_bd = sem("p_bd"); p_fold = sem("p_fold"); p_fhi = sem("p_fhi"); p_flo = sem("p_flo"); p_c16 = sem("p_c16")

        s_bn = sem("s_bn"); s_ag = sem("s_ag"); s_ve = sem("s_ve"); s_rs = sem("s_rs")
        s_tok = sem("s_tok")
        s_tr = sem("s_tr")
        s_hi = sem("s_hi")
        s_lo = sem("s_lo")
        s_sc16 = sem("s_sc16")
        s_wd = sem("s_wd")
        s_bc = sem("s_bc")
        s_bcs = sem("s_bcs")
        s_on = sem("s_on")
        s_onh = sem("s_onh")
        s_onl = sem("s_onl")
        s_qm = sem("s_qm")
        s_pj = sem("s_pj")
        s_tmp = sem("s_tmp")
        s_qk = sem("s_qk")
        s_sph = sem("s_sph")
        s_spl = sem("s_spl")
        s_vp = sem("s_vp")
        s_vs = sem("s_vs")
        s_kt = sem("s_kt")
        s_ktok = sem("s_ktok")
        s_kv = sem("s_kv")
        s_kvm = sem("s_kvm")
        s_sc = sem("s_sc")
        s_st = sem("s_st")
        s_pv = sem("s_pv")
        s_sq = sem("s_sq")
        s_me = sem("s_me")
        s_op = sem("s_op")
        s_res = sem("s_res")
        s_lg = sem("s_lg")
        s_gv = sem("s_gv")
        s_ge = sem("s_ge")
        s_c16 = sem("s_c16")
        s_ctp = sem("s_ctp")
        s_ct = sem("s_ct")
        s_up = sem("s_up")
        s_sg = sem("s_sg")
        s_t1 = sem("s_t1")
        s_h = sem("s_h")
        s_hh = sem("s_hh")
        s_hl = sem("s_hl")
        s_dn = sem("s_dn")
        s_bp = sem("s_bp")
        s_xb = sem("s_xb")
        s_s = sem("s_s")
        s_mx = sem("s_mx"); s_nb = sem("s_nb")
        s_e = sem("s_e")
        s_t = sem("s_t")
        s_pa = sem("s_pa")
        s_pd = sem("s_pd")
        s_pvb = sem("s_pvb")
        s_out = sem("s_out")
        GV = 16
        NS = T * 8

        block = ctx.enter_context(nc.Block())

        @block.sync
        def _(sp):
            sp.dma_start(cst[:, :], consts).then_inc(l_cst, 16)
            sp.dma_start(sel_raw[0], sel_in[:, 0:sel_a]).then_inc(l_cst, 16)
            sp.dma_start(sel_raw[1], sel_in[:, sel_a:FP]).then_inc(l_cst, 16)
            sp.dma_start(wqk_raw, wqk.rearrange("w (h p) i -> p w h i", p=P)).then_inc(l_wa, 16)
            sp.dma_start(fm, fmap).then_inc(l_wa, 16)
            sp.dma_start(vec[:, :], vecs).then_inc(l_wa, 16)
            sp.dma_start(rowb[:, :, :], rows_b).then_inc(s_out, 16)
            for i, (src, _, _, _, _) in enumerate(pieces):
                if i >= NPL:
                    sp.wait_ge(w_lo, i - NPL + 1)
                sp.dma_start(staged(i), src).then_inc(l_pc[i % NPL], 16)
            for b in range(B):
                if b == 0:
                    sp.wait_ge(p_c16, 4)
                else:
                    sp.wait_ge(s_res, 8 * (b - 1) + 2)
                sp.dma_start(xin[:, :, :], x_in[b].rearrange("(t p) d -> p t d", p=P)).then_inc(l_x, 16)
                if b >= 1:
                    sp.wait_ge(s_res, 8 * b)
                    sp.dma_start(out[b - 1].rearrange("(t p) d -> p t d", p=P), x[:, :, :]).then_inc(s_out, 16)
            sp.wait_ge(s_res, 8 * B)
            sp.dma_start(out[B - 1].rearrange("(t p) d -> p t d", p=P), x[:, :, :]).then_inc(s_out, 16)
            sp.wait_ge(s_out, 16 * (B + 1))

        def piece_in(eng, i):
            eng.wait_ge(l_pc[i % NPL], 16 * (i // NPL + 1))

        @block.gpsimd
        def _(pool):
            with pool.Fori(0, B) as b:
                def rsqrt_ln(s):
                    pool.wait_ge(s_ve, b * 4 + (s + 1))
                    nc.gpsimd.tensor_tensor(rstd[:, 0:T], ve[:, 0:T], cst[:, C_HALF:C_HALF + T], ALU.pow).then_inc(s_rs, 1)

                rsqrt_ln(0)
                for c in range(T):
                    if c >= 2:
                        pool.wait_ge(s_wd, b * 8 + (c - 1))
                    pool.wait_ge(s_me, b * T + (c + 1))
                    nc.gpsimd.tensor_tensor(sc16[:, c % 2, :], ve[:, :], cst[:, C_HALF:C_HALF + H], ALU.pow).then_inc(s_sc16, 1)
                rsqrt_ln(1)
                rsqrt_ln(2)
                pool.wait_ge(s_tok, b * (4 * TS) + 12)
                for t in range(T):
                    i = nc.gpsimd.tensor_tensor(x[:, t, :], x[:, t, :], rowb[:, 1, :], ALU.add)
                i.then_inc(s_xb, 1)
                rsqrt_ln(3)

        @block.scalar
        def _(act):
            act.wait_ge(l_wa, 48)
            for w in range(4):
                act.wait_ge(p_fold, w + 1)
                nc.scalar.copy(w_feat[:, 0, w, :, :], bank[:, w, :].rearrange("p (k n) -> p k n", k=KD)).then_inc(p_fhi, 1)
            for i, (_, hi, _, _, factor) in enumerate(pieces):
                piece_in(act, i)
                if factor is None:
                    nc.scalar.copy(hi, staged(i)).then_inc(w_hi, 1)
                else:
                    nc.scalar.activation(hi, staged(i), ACT.Copy, scale=vec[:, factor:factor + 1]).then_inc(w_hi, 1)

            with act.Fori(0, B) as b:
                def split_hi(i):
                    for k in range(KD):
                        act.wait_ge(s_tr, b * (2 * TS) + (2 * i + k + 1))
                        nc.scalar.copy(xt[:, 0, k, :], bank[:, k, :]).then_inc(s_hi, 1)

                def split_qk_hi(stage, n, half, is_q):
                    act.wait_ge(s_qk, b * 8 + (4 * stage + n))
                    if not is_q:
                        nc.scalar.copy(ks[:, 0, half, :], qk[:, half, :]).then_inc(s_sph, 1)
                    else:
                        for odd in range(2):
                            nc.scalar.activation(qs[:, 0, half, odd, :], qk[:, 2 + half, :], ACT.Copy,
                                                 scale=cst[:, C_EVEN + odd:C_EVEN + odd + 1]).then_inc(s_sph, 1)

                def widen(stage, c):
                    act.wait_ge(s_sc16, b * 8 + (4 * stage + c + 1))
                    if stage == 0 and c == 0:
                        act.wait_ge(s_out, b * 16 + 16)
                    if c >= (2, 1)[stage]:
                        act.wait_ge(s_bc, b * 8 + (4 * stage + c - (1, 0)[stage]))
                    nc.scalar.copy(wide_at(stage, c).rearrange("p (h d) -> p h d", d=DK),
                                   sc16[:, c % 2, :, None].broadcast_to([P, H, DK])).then_inc(s_wd, 1)

                def scale_out(stage, c):
                    act.wait_ge(s_bc, b * 8 + (4 * stage + c + 1))
                    if c:
                        act.wait_ge(s_on, b * 8 + (4 * stage + c))
                    o = (4 if stage == 0 else 6) + c % 2
                    nc.scalar.copy(scale, bank[:, o, D:2 * D]).then_inc(s_bcs, 1)

                def high_out(stage, c):
                    act.wait_ge(s_on, b * 8 + (4 * stage + c + 1))
                    cols = slice(c * P, (c + 1) * P)
                    nc.scalar.copy(xt[:, 0, :, cols], on[:, :, cols]).then_inc(s_onh, 1)

                split_hi(0)
                for j in range(4):
                    act.wait_ge(s_pj, b * 4 + (j + 1))
                    if j >= 2:
                        act.wait_ge(s_qk, b * 8 + (j - 1))
                    nc.scalar.activation(work[:, j % 2, :], bank[:, (2 * j + 2) % 8, :], ACT.Identity,
                                         bias=vec[:, (V_K1, V_K1, V_Q1, V_Q1)[j]:(V_K1, V_K1, V_Q1, V_Q1)[j] + 1]
                                         ).then_inc(s_tmp, 1)
                    if j >= 1:
                        split_qk_hi(0, j, (j - 1) % 2, j - 1 >= 2)
                split_qk_hi(0, 4, 1, True)
                for t in range(T):
                    act.wait_ge(s_vp, b * 4 + (t // 2 + 1))
                    nc.scalar.copy(v_at(t, 0, H), bank[:, 2 + t // 2, (t % 2) * D:(t % 2 + 1) * D].rearrange(
                        "p (n a e) -> p n a e", a=2, e=DK)).then_inc(s_vs, 1)
                for i in range(2):
                    act.wait_ge(s_kt, b * 2 + (i + 1))
                    nc.scalar.copy(ktok[:, :, i * P:(i + 1) * P], bank[:, 4 + i, :].rearrange("p (t n) -> p t n", t=T)
                                   ).then_inc(s_ktok, 1)
                for c in range(T):
                    act.wait_ge(s_pv, b * 8 + 2 * (c + 1))
                    if c:
                        act.wait_ge(s_qm, b * T + c)
                    nc.scalar.activation(sq, bank[:, 4 + c % 2, 0:D], ACT.Square).then_inc(s_sq, 1)
                    if c:
                        widen(0, c - 1)
                        scale_out(0, c - 1)
                        high_out(0, c - 1)
                widen(0, T - 1)
                scale_out(0, T - 1)
                high_out(0, T - 1)

                def ffn(f):
                    split_hi(1 if f == 0 else 3)
                    act.wait_ge(s_gv, b * (2 * GV) + (f * GV + 2))
                    nc.scalar.activation(gb[:, :, :], ga[:, :, :], ACT.Exp).then_inc(s_ge, 1)

                    def high(i):
                        act.wait_ge(s_h, b * (2 * FT) + (f * FT + i + 1))
                        if i >= 3:
                            act.wait_ge(s_dn, b * (2 * FT) + (f * FT + i - 2))
                        nc.scalar.copy(hs[:, 2 * (i % 3), :], work[:, 3 + i % 2, :]).then_inc(s_hh, 1)

                    for i in range(FT):
                        act.wait_ge(s_up, b * (2 * FT) + (f * FT + i + 1))
                        nc.scalar.activation(work[:, i % 2, :], bank[:, 4 + i % 2, :], ACT.Silu).then_inc(s_sg, 1)
                        if i >= 1:
                            high(i - 1)
                    high(FT - 1)

                ffn(0)
                split_hi(2)
                for n in range(4):
                    split_qk_hi(1, n + 1, n % 2, n < 2)

                def exps(p):
                    qt, W = p // 8, (p // 8 + 1) * P
                    for i in range(2):
                        if i == 0:
                            act.wait_ge(s_nb, b * NS + (p + 1))
                            if p >= 2:
                                act.wait_ge(s_t, b * NS + (p - 1))
                        rp, hp = p % 2, p % 8 // 2
                        h = head_of(hp // 2, 2 * rp + i, hp % 2)
                        nc.scalar.activation(work[:, 2 * (p % 2) + i, 0:W], bank[:, 2 * rp + i, 0:W], ACT.Exp,
                                             bias=nb[:, p % 2, i:i + 1], scale=DK ** -0.5,
                                             accum_out=sums[:, qt % 2, h:h + 1]).then_inc(s_e, 1)

                def evac(p):
                    W = (p // 8 + 1) * P
                    act.wait_ge(s_t, b * NS + (p + 1))
                    if p >= 2:
                        act.wait_ge(s_pvb, b * NS + (p - 1))
                    nc.scalar.copy(qk[:, 2 * (p % 2), 0:W], bank[:, 4, 0:W]).then_inc(s_pa, 1)

                for p in range(NS + 1):
                    if p < NS:
                        exps(p)
                    if p >= 1:
                        evac(p - 1)
                    if p >= 10 and (p - 2) % 8 == 0:
                        widen(1, (p - 2) // 8 - 1)
                    if p >= 11 and (p - 3) % 8 == 0:
                        scale_out(1, (p - 3) // 8 - 1)
                        high_out(1, (p - 3) // 8 - 1)
                widen(1, T - 1)
                scale_out(1, T - 1)
                high_out(1, T - 1)
                ffn(1)

        @block.vector
        def _(dve):
            dve.wait_ge(l_cst, 48)
            nc.vector.tensor_copy(ident16[:, :], ident).then_inc(p_c16, 1)
            nc.vector.tensor_scalar(neg16[:, :], tri, 1.0, -NEG, ALU.subtract, ALU.mult).then_inc(p_c16, 1)
            nc.vector.tensor_copy(sel16[:, 0:sel_a], sel_raw[0]).then_inc(p_c16, 1)
            nc.vector.tensor_copy(sel16[:, sel_a:FP], sel_raw[1]).then_inc(p_c16, 1)
            nc.vector.memset(c16[:, :, 3 * E:32], 0.0).then_inc(p_c16, 1)
            dve.wait_ge(p_c16, 5)
            nc.vector.memset(c16[:, :, 3 * E:3 * E + 1], 1.0).then_inc(p_c16, 1)
            dve.wait_ge(l_wa, 48)
            for w in range(4):
                src = fm[:, w, None, :].broadcast_to([P, P // DK, DK])
                nc.vector.scalar_tensor_tensor(bd[:, w, :].rearrange("p (h d) -> p h d", d=DK), src, DK ** -0.5 if w == 0 else 1.0,
                                               bdmask.rearrange("p (h d) -> p h d", d=DK), ALU.mult, ALU.mult
                                               ).then_inc(p_bd, 1)
            nc.vector.tensor_scalar(vec[:, V_Q1:V_Q1 + 1], vec[:, V_Q1:V_Q1 + 1], DK ** -0.5, None, ALU.mult).then_inc(p_bd, 1)
            dve.wait_ge(p_bd, 4)
            nc.vector.memset(vp[:, :, :, :, :], 0.0).then_inc(p_c16, 1)
            for w in range(4):
                dve.wait_ge(p_fhi, w + 1)
                nc.vector.tensor_tensor(w_feat[:, 1, w, :, :], bank[:, w, :].rearrange("p (k n) -> p k n", k=KD),
                                        w_feat[:, 0, w, :, :].bitcast(F32), ALU.subtract).then_inc(p_flo, 1)
            for i, (_, hi, lo, _, factor) in enumerate(pieces):
                dve.wait_ge(w_hi, i + 1)
                if factor is None:
                    nc.vector.tensor_tensor(lo, staged(i), hi.bitcast(F32), ALU.subtract).then_inc(w_lo, 1)
                else:
                    nc.vector.scalar_tensor_tensor(lo, staged(i), vec[:, factor:factor + 1], hi.bitcast(F32),
                                                   ALU.mult, ALU.subtract).then_inc(w_lo, 1)
            dve.wait_ge(w_lo, NPC)
            dve.wait_ge(p_c16, 7)

            with dve.Fori(0, B) as b:
                def carry(semaphore, value):
                    dve.wait_ge(semaphore, value)
                    carried[0] += 1
                    nc.vector.tensor_copy(spare[:, carried[0]:carried[0] + 1], cst[:, C_ODD:C_ODD + 1])

                carried = [-1]

                def layernorm(s, i, src):
                    for t in range(T):
                        nc.vector.bn_stats(st6[:, t, :], src[:, t, :]).then_inc(s_bn, 1)
                    carry(s_bn, b * 16 + (4 * s + 4))
                    for t in range(T):
                        nc.vector.bn_aggr(mv[:, t, :], st6[:, t, :]).then_inc(s_ag, 1)
                    dve.wait_ge(s_ag, b * 16 + (4 * s + 4))
                    nc.vector.tensor_scalar(ve[:, 0:T], mv[:, :, 1], EPS, None, ALU.add).then_inc(s_ve, 1)
                    dve.wait_ge(s_rs, b * 4 + (s + 1))
                    for t in range(T):
                        nc.vector.tensor_scalar(xn[:, t, :], src[:, t, :], mv[:, t, 0:1], rstd[:, t:t + 1],
                                                ALU.subtract, ALU.mult).then_inc(s_tok, 1)

                def split_lo(i):
                    for k in range(KD):
                        dve.wait_ge(s_hi, b * (2 * TS) + (2 * i + k + 1))
                        nc.vector.tensor_tensor(xt[:, 1, k, :], bank[:, k, :], xt[:, 0, k, :].bitcast(F32),
                                                ALU.subtract).then_inc(s_lo, 1)

                def split_qk_lo(stage, n, half, is_q):
                    dve.wait_ge(s_sph, b * 12 + (6 * stage + n))
                    if not is_q:
                        nc.vector.tensor_tensor(ks[:, 1, half, :], qk[:, half, :], ks[:, 0, half, :].bitcast(F32),
                                                ALU.subtract).then_inc(s_spl, 1)
                    else:
                        for odd in range(2):
                            nc.vector.scalar_tensor_tensor(qs[:, 1, half, odd, :], qk[:, 2 + half, :],
                                                           cst[:, C_EVEN + odd:C_EVEN + odd + 1],
                                                           qs[:, 0, half, odd, :].bitcast(F32),
                                                           ALU.mult, ALU.subtract).then_inc(s_spl, 1)

                def scaled(stage, c):
                    dve.wait_ge(s_bcs, b * 8 + (4 * stage + c + 1))
                    o = (4 if stage == 0 else 6) + c % 2
                    nc.vector.tensor_tensor(on[:, :, c * P:(c + 1) * P], bank[:, o, 0:D].rearrange("p (k l) -> p k l", k=KD),
                                            scale.rearrange("p (k l) -> p k l", k=KD), ALU.mult).then_inc(s_on, 1)

                def low_out(stage, c):
                    dve.wait_ge(s_onh, b * 8 + (4 * stage + c + 1))
                    cols = slice(c * P, (c + 1) * P)
                    nc.vector.tensor_tensor(xt[:, 1, :, cols], on[:, :, cols], xt[:, 0, :, cols].bitcast(F32),
                                            ALU.subtract).then_inc(s_onl, 1)

                def residual(n, first, base):
                    for i in range(2):
                        nc.vector.tensor_tensor(x[:, 2 * i:2 * i + 2, :], base[:, 2 * i:2 * i + 2, :],
                                                bank[:, first + i, :].rearrange("p (t n) -> p t n", t=2),
                                                ALU.add).then_inc(s_res, 1)
                    dve.wait_ge(s_res, b * 8 + (2 * n + 2))

                dve.wait_ge(l_x, b * 16 + 16)
                layernorm(0, 0, xin)
                split_lo(0)
                for j in range(4):
                    dve.wait_ge(s_tmp, b * 4 + (j + 1))
                    v2 = (V_K2, V_K2, V_Q2, V_Q2)[j]
                    nc.vector.scalar_tensor_tensor(qk[:, j, :], bank[:, (2 * j + 3) % 8, :], vec[:, v2:v2 + 1],
                                                   work[:, j % 2, :], ALU.add, ALU.mult).then_inc(s_qk, 1)
                for n, half, is_q in ((1, 0, False), (2, 1, False), (4, 0, True), (6, 1, True)):
                    split_qk_lo(0, n, half, is_q)

                def scores_out(m):
                    dve.wait_ge(s_sc, b * 8 + (m + 1))
                    if m >= 2:
                        dve.wait_ge(s_pv, b * 8 + (m - 1))
                    for i in range(2):
                        nc.vector.tensor_tensor(work[:, 2 * (m % 2) + i, :].rearrange("p (h c) -> p h c", h=4),
                                                bank[:, 2 * (m % 2) + i, :].rearrange("p (h c) -> p h c", h=4),
                                                tri[:, None, :].broadcast_to([P, 4, P]), ALU.mult).then_inc(s_st, 1)

                def states_out():
                    for i, (lo, hi) in enumerate(((0, 2), (2, 3))):
                        dve.wait_ge(s_kv, b * 2 + (i + 1))
                        n = 2 * (hi - lo)
                        nc.vector.tensor_tensor(kvm[:, lo:hi, :].rearrange("p a (h n) -> p (a h) n", n=P),
                                                bank[:, 6 + i, 0:n * P].rearrange("p (a n) -> p a n", n=P),
                                                bdmask[:, None, :].broadcast_to([P, n, P]), ALU.mult).then_inc(s_kvm, 1)

                def mean_squares(c):
                    dve.wait_ge(s_qm, b * T + (c + 1))
                    if c:
                        dve.wait_ge(s_sc16, b * 8 + c)
                    nc.vector.tensor_scalar(ve[:, :], bank[:, 6 + c % 2, 0:H], 1.0 / DK, EPS, ALU.mult, ALU.add
                                            ).then_inc(s_me, 1)

                scores_out(0)
                states_out()
                for m in range(1, 8):
                    scores_out(m)
                    if m >= 4 and m % 2 == 0:
                        mean_squares(m // 2 - 2)
                    if m >= 5 and m % 2 == 1:
                        scaled(0, (m - 5) // 2)
                        low_out(0, (m - 5) // 2)
                mean_squares(2)
                scaled(0, 2)
                low_out(0, 2)
                mean_squares(3)
                scaled(0, 3)
                low_out(0, 3)
                dve.wait_ge(s_op, b * 4 + 2)
                dve.wait_ge(s_out, b * 16 + 16)
                residual(0, 2, xin)

                def ffn(f):
                    i0 = 1 if f == 0 else 3
                    layernorm(1 if f == 0 else 3, i0, x)
                    split_lo(i0)
                    g = [f * GV]

                    def step(ins, wait=True):
                        g[0] += 1
                        ins.then_inc(s_gv, 1)
                        if wait:
                            dve.wait_ge(s_gv, b * (2 * GV) + g[0])

                    def wide(a):
                        return a.broadcast_to([P, T, E])

                    dve.wait_ge(s_lg, b * 2 + (f + 1))
                    lg = bank[:, 2, 0:T * E].rearrange("p (t e) -> p t e", e=E)
                    step(nc.vector.tensor_reduce(gs[:, 0, :], lg, AX_X, ALU.max))
                    step(nc.vector.tensor_tensor(ga[:, :, :], lg, wide(gs[:, 0, :, None]), ALU.subtract), False)
                    dve.wait_ge(s_ge, b * 2 + (f + 1))
                    step(nc.vector.tensor_reduce(gs[:, 1, :], gb[:, :, :], AX_X, ALU.add))
                    step(nc.vector.reciprocal(gs[:, 2, :], gs[:, 1, :]))
                    step(nc.vector.tensor_tensor(ga[:, :, :], gb[:, :, :], wide(gs[:, 2, :, None]), ALU.mult), False)
                    carry(s_gv, b * (2 * GV) + g[0])
                    for t in range(T):
                        ins = nc.vector.max(gtop[:, t, :], ga[:, t, :])
                    step(ins, False)
                    carry(s_gv, b * (2 * GV) + g[0])
                    for t in range(T):
                        ins = nc.vector.max_index(gidx[:, t, :], gtop[:, t, :], ga[:, t, :])
                    step(ins)
                    step(nc.vector.tensor_copy(gidf[:, :, :], gidx[:, :, 0:2]), False)
                    step(nc.vector.scalar_tensor_tensor(gs[:, 3, :], gtop[:, :, 0], 1e-20, gtop[:, :, 1], ALU.add, ALU.add))
                    step(nc.vector.reciprocal(gs[:, 1, :], gs[:, 3, :]))
                    for j in range(2):
                        nc.vector.tensor_tensor(gw[:, j, :], gtop[:, :, j], gs[:, 1, :], ALU.mult)
                        ins = nc.vector.tensor_tensor(geq[:, j, :, :], iota8[:, None, :].broadcast_to([P, T, E]),
                                                      wide(gidf[:, :, j:j + 1]), ALU.is_equal)
                    step(ins)
                    for j in range(2):
                        ins = nc.vector.tensor_tensor(cmb[:, j, :, :], geq[:, j, :, :], wide(gw[:, j, :, None]), ALU.mult)
                    step(ins)
                    step(nc.vector.tensor_tensor(ga[:, :, :], cmb[:, 0, :, :], cmb[:, 1, :, :], ALU.add))
                    step(nc.vector.tensor_copy(c16[:, :, 0:E], ga[:, :, :]))
                    step(nc.vector.tensor_tensor(cmb[:, 2, :, :], ga[:, :, :], c16[:, :, 0:E], ALU.subtract))
                    step(nc.vector.tensor_copy(c16[:, :, E:2 * E], cmb[:, 2, :, :]))
                    assert g[0] == f * GV + GV
                    nc.vector.tensor_tensor(c16[:, :, 2 * E:3 * E], cmb[:, 2, :, :], c16[:, :, E:2 * E],
                                            ALU.subtract).then_inc(s_c16, 1)

                    def n(i):
                        return b * (2 * FT) + (f * FT + i + 1)

                    def low(i):
                        dve.wait_ge(s_hh, n(i))
                        nc.vector.tensor_tensor(hs[:, 2 * (i % 3) + 1, :], work[:, 3 + i % 2, :],
                                                hs[:, 2 * (i % 3), :].bitcast(F32), ALU.subtract).then_inc(s_hl, 1)

                    for i in range(FT):
                        if i == SHARED_TILES:
                            dve.wait_ge(s_ctp, b * 2 + (f + 1))
                            nc.vector.tensor_copy(ct16, bank[0:32, 3, 0:256].bitcast(BF16)).then_inc(s_ct, 1)
                        dve.wait_ge(s_sg, n(i))
                        if i < SHARED_TILES:
                            nc.vector.tensor_tensor(work[:, 3 + i % 2, :], bank[:, 6 + i % 2, :], work[:, i % 2, :],
                                                    ALU.mult).then_inc(s_h, 1)
                        else:
                            if i > SHARED_TILES:
                                dve.wait_ge(s_h, n(i - 1))
                            nc.vector.tensor_tensor(work[:, 2, :], bank[:, 6 + i % 2, :], work[:, i % 2, :],
                                                    ALU.mult).then_inc(s_t1, 1)
                            dve.wait_ge(s_t1, b * (2 * (FT - SHARED_TILES)) + (f * (FT - SHARED_TILES) + i - SHARED_TILES + 1))
                            nc.vector.tensor_tensor(work[:, 3 + i % 2, :], bank[:, 2 + i % 2, :], work[:, 2, :],
                                                    ALU.mult).then_inc(s_h, 1)
                        if i >= 1:
                            low(i - 1)
                    low(FT - 1)
                    dve.wait_ge(s_dn, n(FT - 1))

                ffn(0)
                residual(1, 0, x)

                layernorm(2, 2, x)
                split_lo(2)
                for n in range(4):
                    dve.wait_ge(s_bp, b * 4 + (n + 1))
                    c = V_BQ + n
                    nc.vector.scalar_tensor_tensor(qk[:, (2 + n) % 4, :], bank[:, 2 + n, :], vec[:, c:c + 1], emb,
                                                   ALU.add, ALU.mult).then_inc(s_qk, 1)
                for t in range(T):
                    dve.wait_ge(s_vp, b * 4 + (2 + t // 2 + 1))
                    nc.vector.tensor_tensor(v_at(t, 0, H), bank[:, 6 + t // 2, (t % 2) * D:(t % 2 + 1) * D].rearrange(
                        "p (n a e) -> p n a e", a=2, e=DK), rowb[:, 0, :].rearrange("p (n a e) -> p n a e", a=2, e=DK),
                                            ALU.add).then_inc(s_vs, 1)
                for n, half, is_q in ((2, 0, True), (4, 1, True), (5, 0, False), (6, 1, False)):
                    split_qk_lo(1, n, half, is_q)

                def maxima(p):
                    W = (p // 8 + 1) * P
                    r = 2 * (p % 2)
                    dve.wait_ge(s_s, b * NS + (p + 1))
                    if p >= 2:
                        dve.wait_ge(s_e, b * (2 * NS) + (2 * p - 2))
                    nc.vector.tensor_reduce(mx[:, p % 2, :], bank[:, r:r + 2, 0:W], AX_X, ALU.max).then_inc(s_mx, 1)
                    dve.wait_ge(s_mx, b * NS + (p + 1))
                    nc.vector.tensor_scalar(nb[:, p % 2, :], mx[:, p % 2, :], -(DK ** -0.5), None, ALU.mult).then_inc(s_nb, 1)

                def evac(p):
                    W = (p // 8 + 1) * P
                    dve.wait_ge(s_t, b * NS + (p + 1))
                    if p >= 2:
                        dve.wait_ge(s_pvb, b * NS + (p - 1))
                    nc.vector.tensor_copy(qk[:, 2 * (p % 2) + 1, 0:W], bank[:, 5, 0:W]).then_inc(s_pd, 1)

                def inverse_sums(qt):
                    dve.wait_ge(s_e, b * (2 * NS) + 16 * (qt + 1))
                    if qt >= 2:
                        dve.wait_ge(s_wd, b * 8 + (4 + qt - 1))
                    nc.vector.reciprocal(sc16[:, qt % 2, :], sums[:, qt % 2, :]).then_inc(s_sc16, 1)

                for p in range(NS + 1):
                    if p < NS:
                        maxima(p)
                    if 1 <= p <= NS:
                        evac(p - 1)
                    if p >= 9 and (p - 1) % 8 == 0:
                        inverse_sums((p - 1) // 8 - 1)
                    if p >= 11 and (p - 3) % 8 == 0:
                        scaled(1, (p - 3) // 8 - 1)
                        low_out(1, (p - 3) // 8 - 1)
                inverse_sums(T - 1)
                scaled(1, T - 1)
                low_out(1, T - 1)
                dve.wait_ge(s_op, b * 4 + 4)
                dve.wait_ge(s_xb, b + 1)
                residual(2, 2, x)
                ffn(1)
                residual(3, 0, x)

        @block.tensor
        def _(pe):
            pe.wait_ge(l_cst, 48)
            for w in range(4):
                pe.wait_ge(p_bd, w + 1)
                for k in range(KD):
                    for half in range(KD):
                        ins = nc.tensor.matmul(bank[:, w, (2 * k + half) * P:(2 * k + half + 1) * P],
                                               wqk_raw[:, w // 2, half, k * P:(k + 1) * P], bd[:, w, :],
                                               start=True, stop=True)
                ins.then_inc(p_fold, 1)
            pe.wait_ge(p_flo, 4)
            pe.wait_ge(w_lo, NPC)
            pe.wait_ge(p_c16, 7)

            with pe.Fori(0, B) as b:
                PASSES = ((0, 0), (1, 0), (0, 1))

                def transposed(i):
                    for t in range(T):
                        pe.wait_ge(s_tok, b * (4 * TS) + (4 * i + t + 1))
                        for k in range(KD):
                            ins = nc.tensor.matmul(bank[:, k, t * P:(t + 1) * P], xn[:, t, k * P:(k + 1) * P], ident,
                                                   start=True, stop=True, is_transpose=True)
                            if t == T - 1:
                                ins.then_inc(s_tr, 1)

                def ready(i):
                    pe.wait_ge(s_lo, b * (2 * TS) + (2 * i + 2))

                def by_feature(dst, weight):
                    for n, (k, (a, c)) in enumerate((k, ac) for k in range(KD) for ac in PASSES):
                        ins = nc.tensor.matmul(dst, weight(a, k), xt[:, c, k, :], start=(n == 0), stop=(n == 3 * KD - 1))
                    return ins

                def by_token(dst, t, weight, first):
                    for n, (k, (a, c)) in enumerate((k, ac) for k in range(KD) for ac in PASSES):
                        ins = nc.tensor.matmul(dst, xt[:, a, k, t * P:(t + 1) * P], weight(c, k),
                                               start=(first and n == 0), stop=(n == 3 * KD - 1), skip_group_check=True)
                    return ins

                def two_banks(first, weight, done, before=lambda t: None):
                    for t in range(T):
                        before(t)
                        ins = by_token(bank[:, first + t // 2, (t % 2) * D:(t % 2 + 1) * D], t, weight, t % 2 == 0)
                        if t % 2:
                            ins.then_inc(done, 1)

                transposed(0)
                ready(0)
                for j in range(4):
                    half, pair = j % 2, (2, 2, 0, 0)[j]
                    for i in range(2):
                        ins = by_feature(bank[:, (2 * j + 2 + i) % 8, :],
                                         lambda a, k: w_feat[:, a, pair + i, k, half * P:(half + 1) * P])
                    ins.then_inc(s_pj, 1)
                pe.wait_ge(s_qk, b * 8 + 1)
                two_banks(2, lambda c, k: w_v[:, c, k, :], s_vp)
                for half in range(KD):
                    pe.wait_ge(s_qk, b * 8 + 2)
                    for t in range(T):
                        ins = nc.tensor.matmul(bank[:, 4 + half, t * P:(t + 1) * P], qk[:, half, t * P:(t + 1) * P],
                                               ident, start=True, stop=True, is_transpose=True)
                    ins.then_inc(s_kt, 1)

                def scores(m):
                    c = m // 2
                    if m >= 2:
                        pe.wait_ge(s_st, b * 16 + 2 * (m - 1))
                    cols = slice(c * P, (c + 1) * P)
                    for half in range(KD):
                        for n, (a, q) in enumerate(PASSES):
                            for i in range(2):
                                rows = slice(32 * (2 * (m % 2) + i), 32 * (2 * (m % 2) + i) + 32)
                                ins = nc.tensor.matmul(bank[:, 2 * (m % 2) + i, half * 2 * P:(half + 1) * 2 * P],
                                                       ks[rows, a, half, cols], qs[rows, q, half, :, cols],
                                                       start=(n == 0), stop=(n == 2))
                    ins.then_inc(s_sc, 1)

                def states():
                    pe.wait_ge(s_ktok, b * 2 + 2)
                    pe.wait_ge(s_vs, b * (2 * T) + T)
                    for n in range(1, T):
                        for half in range(KD):
                            cols = slice(half * P, (half + 1) * P)
                            at = ((n - 1) % 2) * D + half * P
                            for c in range(n):
                                ins = nc.tensor.matmul(bank[:, 6 + (n - 1) // 2, at:at + P], ktok[:, c, cols],
                                                       v_at(c, 8 * half, 8 * half + 8), start=(c == 0), stop=(c == n - 1))
                        if n >= 2:
                            ins.then_inc(s_kv, 1)

                def products(m):
                    c, o = m // 2, 4 + m // 2 % 2
                    if m % 2 == 0:
                        if c == 1:
                            pe.wait_ge(s_kvm, b * 2 + 2)
                        if c >= 2:
                            pe.wait_ge(s_on, b * 8 + (c - 1))
                        if c:
                            for half in range(KD):
                                cols = slice(half * P, (half + 1) * P)
                                nc.tensor.matmul(bank[:, o, cols], kvm[:, c - 1, cols], qk[:, 2 + half, c * P:(c + 1) * P],
                                                 start=(half == 0), stop=False, skip_group_check=True)
                    pe.wait_ge(s_st, b * 16 + 2 * (m + 1))
                    for hp in range(4):
                        half, odd = hp // 2, hp % 2
                        for i in range(2):
                            r = 2 * (m % 2) + i
                            ins = nc.tensor.matmul(bank[32 * r:32 * r + 32, o, half * P:(half + 1) * P],
                                                   vp[:, c, half * 4 + r, 2 * odd:2 * odd + 2, :],
                                                   work[:, r, hp * P:(hp + 1) * P],
                                                   start=(c == 0 and odd == 0), stop=(odd == 1), skip_group_check=True,
                                                   tile_position=(0, 32 * r))
                    ins.then_inc(s_pv, 1)

                def squares_summed(c):
                    pe.wait_ge(s_sq, b * T + (c + 1))
                    if c >= 2:
                        pe.wait_ge(s_me, b * T + (c - 1))
                    for half in range(KD):
                        ins = nc.tensor.matmul(bank[:, 6 + c % 2, half * 8:half * 8 + 8], sq[:, half * P:(half + 1) * P],
                                               bdmask[:, 0:P:DK], start=(half == 0), stop=True, skip_group_check=True)
                    ins.then_inc(s_qm, 1)

                def scales_turned(stage, c):
                    o = (4 if stage == 0 else 6) + c % 2
                    pe.wait_ge(s_wd, b * 8 + (4 * stage + c + 1))
                    for half in range(KD):
                        ins = nc.tensor.matmul(bank[:, o, D + half * P:D + (half + 1) * P],
                                               wide_at(stage, c)[:, half * P:(half + 1) * P], ident,
                                               start=True, stop=True, is_transpose=True)
                    ins.then_inc(s_bc, 1)

                def outputs_ready(stage):
                    return lambda t: pe.wait_ge(s_onl, b * 8 + (4 * stage + t + 1))

                pe.wait_ge(s_qk, b * 8 + 4)
                pe.wait_ge(s_spl, b * 12 + 6)
                scores(0)
                states()
                scores(1)
                for m in range(8):
                    products(m)
                    if m + 2 < 8:
                        scores(m + 2)
                    if m >= 2 and m % 2 == 0:
                        squares_summed(m // 2 - 1)
                    if m >= 3 and m % 2 == 1:
                        scales_turned(0, m // 2 - 1)
                squares_summed(3)
                scales_turned(0, 3)
                two_banks(2, lambda c, k: w_o[:, c, k, :], s_op, outputs_ready(0))

                def ffn(f):
                    i0 = 1 if f == 0 else 3
                    transposed(i0)
                    ready(i0)
                    for t in range(T):
                        ins = by_token(bank[:, 2, t * E:(t + 1) * E], t, lambda c, k: w_gate[:, c, k, :], t == 0)
                    ins.then_inc(s_lg, 1)

                    def n(i):
                        return b * (2 * FT) + (f * FT + i + 1)

                    def up(i):
                        cols = slice(i * P, (i + 1) * P)
                        if i >= 2:
                            pe.wait_ge(s_h, n(i - 2))
                        for g in range(2):
                            ins = by_feature(bank[:, 4 + 2 * g + i % 2, :], lambda a, k: w_gu[:, a, g, k, cols])
                        if i == SHARED_TILES:
                            pe.wait_ge(s_c16, b * 2 + (f + 1))
                            for t in range(T):
                                ins = nc.tensor.matmul(bank[0:32, 3, t * 64:(t + 1) * 64].bitcast(BF16), c16[:, t, :],
                                                       ident16[:, :], start=True, stop=True, is_transpose=True)
                            ins.then_inc(s_ctp, 1)
                            pe.wait_ge(s_ct, b * 2 + (f + 1))
                        if i >= SHARED_TILES:
                            ins = nc.tensor.matmul(bank[:, 2 + i % 2, :], sel16[:, cols], ct16, start=True, stop=True)
                        ins.then_inc(s_up, 1)

                    def down(i):
                        pe.wait_ge(s_hl, n(i))
                        s = 2 * (i % 3)
                        for t in range(T):
                            for a, c in PASSES:
                                ins = nc.tensor.matmul(bank[:, t // 2, (t % 2) * D:(t % 2 + 1) * D],
                                                       hs[:, s + a, t * P:(t + 1) * P], w_dn[:, c, i, :],
                                                       start=(i == 0 and t % 2 == 0 and a == 0 and c == 0),
                                                       stop=(i == FT - 1), skip_group_check=True)
                        ins.then_inc(s_dn, 1)

                    for i in range(FT + 2):
                        if i < FT:
                            up(i)
                        if i >= 2:
                            down(i - 2)

                ffn(0)

                transposed(2)
                ready(2)
                for n in range(4):
                    ins = by_feature(bank[:, 2 + n, :], lambda a, k: w_qkv[:, a, k, n * P:(n + 1) * P])
                    ins.then_inc(s_bp, 1)
                two_banks(6, lambda c, k: w_qkv[:, c, k, 2 * D:3 * D], s_vp)
                pe.wait_ge(s_vs, b * (2 * T) + 2 * T)
                pe.wait_ge(s_qk, b * 8 + 8)
                pe.wait_ge(s_spl, b * 12 + 12)

                def scores_b(p):
                    qt, rp, hp = p // 8, p % 2, p % 8 // 2
                    W, half, odd = (qt + 1) * P, hp // 2, hp % 2
                    if p >= 2:
                        pe.wait_ge(s_e, b * (2 * NS) + (2 * p - 2))
                    for i in range(2):
                        nc.tensor.matmul(bank[:, 2 * rp + i, qt * P:W], neg16[:, :], ident16[:, :],
                                         start=True, stop=False, skip_group_check=True)
                    for n, (a, c) in enumerate(PASSES):
                        for i in range(2):
                            rows = slice(32 * (2 * rp + i), 32 * (2 * rp + i) + 32)
                            ins = nc.tensor.matmul(bank[:, 2 * rp + i, 0:W], qs[rows, a, half, odd, qt * P:W],
                                                   ks[rows, c, half, 0:W], start=False, stop=(n == 2),
                                                   skip_group_check=True)
                    ins.then_inc(s_s, 1)

                def turn(p):
                    qt = p // 8
                    pe.wait_ge(s_e, b * (2 * NS) + (2 * p + 2))
                    if p >= 1:
                        pe.wait_ge(s_pa, b * NS + p)
                        pe.wait_ge(s_pd, b * NS + p)
                    for i in range(2):
                        for kb in range(qt + 1):
                            ins = nc.tensor.matmul(bank[:, 4 + i, kb * P:(kb + 1) * P],
                                                   work[:, 2 * (p % 2) + i, kb * P:(kb + 1) * P], ident,
                                                   start=True, stop=True, is_transpose=True)
                    ins.then_inc(s_t, 1)

                def products_b(p):
                    qt, rp, hp = p // 8, p % 2, p % 8 // 2
                    half, odd, o = hp // 2, hp % 2, 6 + qt % 2
                    pe.wait_ge(s_pa, b * NS + (p + 1))
                    pe.wait_ge(s_pd, b * NS + (p + 1))
                    if p % 8 == 0 and qt >= 2:
                        pe.wait_ge(s_on, b * 8 + (4 + qt - 1))
                    for i in range(2):
                        r = 2 * rp + i
                        for kb in range(qt + 1):
                            ins = nc.tensor.matmul(bank[32 * r:32 * r + 32, o, half * P:(half + 1) * P],
                                                   vp[:, kb, half * 4 + r, 2 * odd:2 * odd + 2, :],
                                                   qk[:, 2 * (p % 2) + i, kb * P:(kb + 1) * P],
                                                   start=(odd == 0 and kb == 0), stop=(odd == 1 and kb == qt),
                                                   skip_group_check=True, tile_position=(0, 32 * r))
                    ins.then_inc(s_pvb, 1)

                for p in range(NS + 2):
                    if p < NS:
                        scores_b(p)
                    if p >= 2:
                        products_b(p - 2)
                    if 1 <= p <= NS:
                        turn(p - 1)
                    if p >= 10 and (p - 2) % 8 == 0:
                        scales_turned(1, (p - 2) // 8 - 1)
                scales_turned(1, T - 1)
                two_banks(2, lambda c, k: w_out[:, c, k, :], s_op, outputs_ready(1))
                ffn(1)


def _layout(n):
    def tiled(a):
        return np.tile(a, P // DK)

    pad = np.zeros((FP - F, D), np.float32)
    wide = {k: np.asarray(a) for k, a in n.items()}
    gate = np.concatenate([wide["L0_ffn_shared_gate"], wide["L0_ffn_expert_gate"].reshape(E * I, D), pad])
    up = np.concatenate([wide["L0_ffn_shared_up"], wide["L0_ffn_expert_up"].reshape(E * I, D), pad])
    down = np.concatenate([wide["L0_ffn_shared_down"].T,
                           wide["L0_ffn_expert_down"].transpose(0, 2, 1).reshape(E * I, D), pad])
    qkv_b = wide["L0_attn_b_qkv_b"]
    maps = [wide[f"L0_attn_a_{k}_w"] for k in ("fq1", "fq2", "fk1", "fk2")]
    vecs = [tiled(wide[f"L0_attn_a_{k}"]) for k in ("fq1_b", "fq2_b", "fk1_b", "fk2_b", "norm_w")]
    vecs += [qkv_b[i * P:(i + 1) * P] for i in range(4)]
    rows = np.stack([qkv_b[2 * D:3 * D], wide["L0_attn_b_out_b"]])
    return {
        "x": wide["L0_attn_a_x"],
        "wqk": np.stack([wide["L0_attn_a_wq"], wide["L0_attn_a_wk"]]),
        "wv_t": wide["L0_attn_a_wv"].T,
        "wo_t": wide["L0_attn_a_wo"].T,
        "fmap": np.stack([np.tile(m.T, (P // DK, 1)) for m in maps], axis=1),
        "vecs": np.stack(vecs, axis=1),
        "qkv_t": wide["L0_attn_b_qkv_w"].T,
        "out_t": wide["L0_attn_b_out_w"].T,
        "rows_b": np.broadcast_to(rows, (P, 2, D)),
        "gate_t": wide["L0_ffn_gate_w"].T,
        "gu_t": np.stack([gate.T, up.T], axis=1),
        "down_t": down,
        "consts": _constants(),
        "sel": _selector(),
    }


def _constants():
    r = np.arange(P)
    c = np.zeros((P, C_END), np.float32)
    c[:, C_ID:C_ID + P] = r[:, None] == r[None, :]
    c[:, C_TRI:C_TRI + P] = r[:, None] <= r[None, :]
    c[:, C_BD:C_BD + P] = r[:, None] // DK == r[None, :] // DK
    c[:, C_EVEN] = r // DK % 2 == 0
    c[:, C_ODD] = r // DK % 2 == 1
    c[:, C_IOTA:C_IOTA + E] = np.arange(E)
    c[:, C_HALF:C_HALF + H] = -0.5
    freqs = np.arange(0, DK, 2, dtype=np.float32) / np.float32(DK)
    angles = np.arange(L, dtype=np.float32)[:, None] * freqs[None, :]
    emb = np.concatenate([np.sin(angles), np.cos(angles)], axis=-1)
    c[:, C_EMB:C_EMB + L] = np.tile(emb.T, (P // DK, 1))
    return c


def _selector():
    s = np.zeros((32, FP), np.float32)
    for j in range(FP):
        if ISH <= j < F:
            for part in range(3):
                s[part * E + (j - ISH) // I, j] = 1.0
        else:
            s[3 * E, j] = 1.0
    return s


def kernel(**inputs):
    import concourse.bacc as bacc
    from concourse.bass_utils import run_bass_kernel_spmd

    nc = bacc.Bacc("TRN2", target_bir_lowering=False, num_devices=1)
    arrays, args = {}, []
    for name, a in _layout(inputs).items():
        a = np.ascontiguousarray(a)
        arrays[f"in_{name}"] = a
        args.append(nc.dram_tensor(f"in_{name}", a.shape, mybir.dt.from_np(a.dtype), kind="ExternalInput").ap())
    args.append(nc.dram_tensor("out_0", (B, L, D), F32, kind="ExternalOutput").ap())
    build(nc, *args)
    r = run_bass_kernel_spmd(nc, [arrays], core_ids=[0])
    return r.results[0]["out_0"]
```

```python
from contextlib import ExitStack

import numpy as np

import concourse.bass as bass
from concourse import mybir

ALU = mybir.AluOpType
ACT = mybir.ActivationFunctionType
AX_X = mybir.AxisListType.X
F32 = mybir.dt.float32
F32R = mybir.dt.float32r
BF16 = mybir.dt.bfloat16
U32 = mybir.dt.uint32

P = 128
B, L, D = 4, 512, 256
T = L // P
KD = D // P
H = 16
DK = D // H
EPS = 1e-5
E, I, ISH = 8, 176, 352
LEAD = 32
FP = LEAD + ISH + E * I
FT = FP // P
SHARED = LEAD + ISH
SHARED_TILES = SHARED // P
CH = FP // 2
TS = 5
NEG = -1e30

C_ID, C_TRI, C_BD, C_EVEN, C_ODD, C_IOTA = 0, P, 2 * P, 3 * P, 3 * P + 1, 3 * P + 2
C_HALF = C_IOTA + E
C_ONE = C_HALF + H
C_DIAG = C_ONE + 1
C_EMB = C_DIAG + 2 * DK
C_END = C_EMB + L
V_Q1, V_Q2, V_K1, V_K2, V_NW, V_BQ, V_BK, V_END = 0, 1, 2, 3, 4, 5, 7, 9


SHIFT = 3 * DK
NT = H // 2
NJ = 6
QUERY_JOBS = (((0, 3, 0),), ((1, 3, 0),), ((0, 2, 0), (0, 0, 384)), ((1, 2, 0), (1, 0, 384)), ((0, 1, 0),), ((1, 1, 0),))
KEY_JOBS = (((0, 0, 0),), ((1, 0, 0),), ((0, 3, 0), (0, 1, 128)), ((1, 3, 0), (1, 1, 128)), ((0, 2, 0),), ((1, 2, 0),))

HALF_DONE = (NT // 2 + 2, NT)


def slot(y):
    return min(y, 4), (y == 5) * 2 * P, 4 * P if y < 4 else 2 * P


def diagonals(jobs, by_key):
    starts = sorted(c if by_key else c + t * P for _, t, c in jobs)
    return starts[0], len(starts)


def ring_jobs():
    phases = {}
    for tau in range(-3, NT + 1):
        jobs = []
        if 0 <= tau + 1 < NT:
            jobs.append(("shift", tau + 1))
        if 0 <= tau + 2 < NT:
            jobs += [("scores", tau + 2, n) for n in range(NJ)]
        if tau + 3 < NT:
            jobs += [("stack", tau + 3, op) for op in range(2)]
        if tau >= 2 and tau % 2 == 0:
            jobs.append(("outputs", tau // 2 - 1))
        if tau in HALF_DONE:
            jobs.append(("half", HALF_DONE.index(tau)))
        phases[tau] = jobs
    return phases


RING = ring_jobs()
ORDER = [job for tau in sorted(RING) for job in RING[tau]]
RING_AT = {job: i for i, job in enumerate(ORDER)}
NR = len(RING_AT)
NSTACK = 2 * NT


def ring_read(job):
    def by_scalar(j):
        return j[0] == "stack"
    return by_scalar(job), sum(RING_AT[j] <= RING_AT[job] and by_scalar(j) == by_scalar(job) for j in RING_AT)


def build(nc, x_in, wqk, wv_t, wo_t, fmap, vecs, qkv_t, out_t, rows_b, gu_t, down_t, consts, sel_in, out):
    ctx = ExitStack()
    with ctx:
        def sb(name, shape, dt=F32):
            return ctx.enter_context(nc.sbuf_tensor(name, shape, dt))

        def sem(name):
            return ctx.enter_context(nc.semaphore(name))

        w_feat = sb("w_feat", [P, 2, 4, KD, D], F32R)
        w_v = sb("w_v", [P, 2, KD, D], F32R)
        w_o = sb("w_o", [P, 2, KD, D], F32R)
        w_qkv = sb("w_qkv", [P, 2, KD, 3 * D], F32R)
        w_out = sb("w_out", [P, 2, KD, D], F32R)
        w_gu = sb("w_gu", [P, 2, 2, KD, FP], F32R)
        w_dn = sb("w_dn", [P, 2, FT, D], F32R)
        cst = sb("cst", [P, C_END])
        ident = cst[:, C_ID:C_ID + P]
        tri = cst[:, C_TRI:C_TRI + P]
        bdmask = cst[:, C_BD:C_BD + P]
        iota8 = cst[:, C_IOTA:C_IOTA + E]
        emb = cst[:, C_EMB:C_EMB + L]
        ident16 = sb("ident16", [P, P], BF16)
        neg16 = sb("neg16", [P, P], BF16)
        sel16 = sb("sel16", [32, FP - SHARED], BF16)
        vec = sb("vec", [P, V_END])
        rowb = sb("rowb", [P, 2, D])
        xin = sb("xin", [P, T, D])
        x = sb("x", [P, T, D])
        xn = sb("xn", [P, T, D])
        xt = sb("xt", [P, 2, KD, L], F32R)
        qk = sb("qk", [P, 4, L])
        ks = sb("ks", [P, 2, KD, L], F32R)
        big = sb("big", [P, 8 * L + DK], F32R)
        qs = big[:, 0:8 * L].rearrange("p (a b c l) -> p a b c l", a=2, b=KD, c=2)
        hs = big[:, 0:6 * L].rearrange("p (a l) -> p a l", a=6)
        vp = sb("vp", [P, T, H // 2, 4, DK])
        work = sb("work", [P, 5, L])
        kvm = sb("kvm", [P, 3, D])
        kflat = kvm[:, :, :].rearrange("p a n -> p (a n)")
        ktok = xn
        sq = work[:, 4, 0:D]
        on = xn[:, :, :].rearrange("p a l -> p (a l)").rearrange("p (k l) -> p k l", k=KD)
        wqk_raw = x[:, :, :].rearrange("p (w h) i -> p w h i", w=2)
        bd = work[:, 4, :].rearrange("p (w n) -> p w n", w=4)
        sel_a, sel_n = 1024, FP - SHARED
        sel_raw = (xin[0:32, :, :].rearrange("p a l -> p (a l)"), kflat[0:32, 0:sel_n - sel_a])
        st6 = sb("st6", [P, T, 6])
        mv = sb("mv", [P, T, 2])
        ve = sb("ve", [P, H])
        rstd = sb("rstd", [P, T])
        sc16 = sb("sc16", [P, 2, H])
        mx = sb("mx", [P, 2, T])
        stack = big[:, 0:6 * L].rearrange("p (a c l) -> p a c l", a=3, c=2)
        spread = big[:, 6 * L:6 * L + (4 * 16 + 1) * DK]
        probs = work
        raw = xin[:, :, :].rearrange("p (a t) l -> p a (t l)", a=2)
        shifts = kflat[:, 0:L].rearrange("p (t n) -> p t n", t=T)

        def small(slot, n, dt=F32):
            a = kflat[:, slot * T * E:(slot + n) * T * E].bitcast(dt)
            return a.rearrange("p (t e) -> p t e", t=T) if n == 1 else a.rearrange("p (n t e) -> p n t e", n=n, t=T)

        ga, gb, gtop, gidx, geq, cmb = small(0, 1), small(1, 1), small(2, 1), small(3, 1, U32), small(4, 2), small(6, 3)
        logits = qk[:, 0, :]
        gidf = sb("gidf", [P, T, 2])
        gs = sb("gs", [P, 4, T])
        gw = sb("gw", [P, 2, T])
        c16 = sb("c16", [P, T, 32], BF16)
        ct16 = kflat[0:32, 12 * T * E:12 * T * E + L // 2].bitcast(BF16)
        spare = sb("spare", [P, 12])
        fm = vp[:, 0, 0, :, :]
        wflat = work[:, :, :].rearrange("p a l -> p (a l)")
        qflat = qk[:, :, :].rearrange("p a l -> p (a l)")
        bank = ctx.enter_context(nc.psum_tensor("bank", [P, 8, 512], F32))
        places = [wflat[:, 0:CH], wflat[:, CH:2 * CH], qflat[:, 0:CH], qflat[:, CH:2 * CH]]

        l_cst = sem("l_cst")
        l_wa = sem("l_wa")
        l_x = sem("l_x")
        pieces = [(wv_t, w_v, None), (wo_t, w_o, V_NW), (out_t, w_out, None)]
        pieces = [(s.rearrange("(k p) n -> p k n", p=P), w[:, 0], w[:, 1], (KD, s.shape[1]), f) for s, w, f in pieces]
        for k in range(KD):
            pieces.append((qkv_t[k * P:(k + 1) * P, :], w_qkv[:, 0, k, :], w_qkv[:, 1, k, :], (3 * D,), None))
        for g in range(2):
            for k in range(KD):
                for c in range(2):
                    s = slice(c * CH, (c + 1) * CH)
                    pieces.append((gu_t[k * P:(k + 1) * P, g, s], w_gu[:, 0, g, k, s], w_gu[:, 1, g, k, s], (CH,), None))
        for n0 in range(0, FT, 3):
            n1 = min(FT, n0 + 3)
            pieces.append((down_t.rearrange("(n p) o -> p n o", p=P)[:, n0:n1, :], w_dn[:, 0, n0:n1, :],
                           w_dn[:, 1, n0:n1, :], (n1 - n0, D), None))
        NPC, NPL = len(pieces), len(places)
        FIRST, TURN = 3, 5

        def wide_at(c):
            return x[:, 2 + c % 2, :]

        def v_at(t, h0, h1):
            return vp[:, t, h0 // 2:h1 // 2, 0:4:3, :]

        def staged(i):
            shape = pieces[i][3]
            n = int(np.prod(shape))
            a = places[i % NPL][:, 0:n]
            return a if len(shape) == 1 else a.rearrange("p (a n) -> p a n", a=shape[0])

        l_pc = [sem(f"l_pc{i}") for i in range(NPL)]
        w_hi = sem("w_hi")
        w_lo = sem("w_lo")
        p_bd = sem("p_bd")
        p_fold = sem("p_fold")
        p_fhi = sem("p_fhi")
        p_flo = sem("p_flo")
        p_c16 = sem("p_c16")

        s_bn = sem("s_bn")
        s_ag = sem("s_ag")
        s_ve = sem("s_ve")
        s_rs = sem("s_rs")
        s_tok = sem("s_tok")
        s_tr = sem("s_tr")
        s_hi = sem("s_hi")
        s_lo = sem("s_lo")
        s_sc16 = sem("s_sc16")
        s_wd = sem("s_wd")
        s_bc = sem("s_bc")
        s_oc = sem("s_oc")
        s_on = sem("s_on")
        s_onh = sem("s_onh")
        s_onl = sem("s_onl")
        s_qm = sem("s_qm")
        s_pj = sem("s_pj")
        s_tmp = sem("s_tmp")
        s_qk = sem("s_qk")
        s_sph = sem("s_sph")
        s_spl = sem("s_spl")
        s_vp = sem("s_vp")
        s_vs = sem("s_vs")
        s_kt = sem("s_kt")
        s_ktok = sem("s_ktok")
        s_kv = sem("s_kv")
        s_kvm = sem("s_kvm")
        s_sc = sem("s_sc")
        s_st = sem("s_st")
        s_pv = sem("s_pv")
        s_sq = sem("s_sq")
        s_me = sem("s_me")
        s_op = sem("s_op")
        s_res = sem("s_res")
        s_lc = sem("s_lc")
        s_lg = sem("s_lg")
        s_gv = sem("s_gv")
        s_ge = sem("s_ge")
        s_c16 = sem("s_c16")
        s_ctp = sem("s_ctp")
        s_ct = sem("s_ct")
        s_up = sem("s_up")
        s_sg = sem("s_sg")
        s_t1 = sem("s_t1")
        s_h = sem("s_h")
        s_hh = sem("s_hh")
        s_hl = sem("s_hl")
        s_dh = sem("s_dh")
        s_dn = sem("s_dn")
        s_bp = sem("s_bp")
        s_xb = sem("s_xb")
        s_bh = sem("s_bh")
        s_bl = sem("s_bl")
        s_pool = sem("s_pool")
        s_one = sem("s_one")
        s_x = sem("s_x")
        s_xf = sem("s_xf")
        s_xa = sem("s_xa")
        s_mx = sem("s_mx")
        s_sh = sem("s_sh")
        s_k = sem("s_k")
        s_e = sem("s_e")
        s_pvb = sem("s_pvb")
        s_u = sem("s_u")
        s_rc = sem("s_rc")
        s_out = sem("s_out")
        TURNED = ((4, 6), (0, 1), (0, 1), (0, 1), (0, 1), (4, 6))
        GV = 16

        block = ctx.enter_context(nc.Block())

        @block.sync
        def _(sp):
            sp.dma_start(cst[:, :], consts).then_inc(l_cst, 16)
            sp.dma_start(sel_raw[0], sel_in[:, 0:sel_a]).then_inc(l_cst, 16)
            sp.dma_start(sel_raw[1], sel_in[:, sel_a:sel_n]).then_inc(l_cst, 16)
            sp.dma_start(wqk_raw, wqk.rearrange("w (h p) i -> p w h i", p=P)).then_inc(l_wa, 16)
            sp.dma_start(fm, fmap).then_inc(l_wa, 16)
            sp.dma_start(vec[:, :], vecs).then_inc(l_wa, 16)
            sp.dma_start(rowb[:, :, :], rows_b).then_inc(s_out, 16)
            for i, (src, _, _, _, _) in enumerate(pieces):
                if i == FIRST:
                    sp.wait_ge(p_c16, 5)
                    sp.dma_start(xin[:, :, :], x_in[0].rearrange("(t p) d -> p t d", p=P)).then_inc(l_x, 16)
                if i >= NPL:
                    sp.wait_ge(w_lo, i - NPL + 1)
                sp.dma_start(staged(i), src).then_inc(l_pc[i % NPL], 16)
            for b in range(B):
                sp.wait_ge(s_res, 8 * b + 6)
                sp.dma_start(xin[:, :, :], x_in[min(b + 1, B - 1)].rearrange("(t p) d -> p t d", p=P)).then_inc(l_x, 16)
                if b < B - 1:
                    sp.wait_ge(s_res, 8 * b + 8)
                    sp.dma_start(out[b].rearrange("(t p) d -> p t d", p=P), x[:, :, :]).then_inc(s_out, 16)
            sp.wait_ge(s_res, 8 * B)
            sp.dma_start(out[B - 1].rearrange("(t p) d -> p t d", p=P), x[:, :, :]).then_inc(s_out, 16)
            sp.wait_ge(s_out, 16 * (B + 1))

        def piece_in(eng, i):
            eng.wait_ge(l_pc[i % NPL], 16 * (i // NPL + 1))

        @block.gpsimd
        def _(pool):
            def rsqrt_ln(b, s):
                for h in range(2):
                    tt = slice(2 * h, 2 * h + 2)
                    pool.wait_ge(s_ve, b * 8 + (2 * s + h + 1))
                    nc.gpsimd.tensor_tensor(rstd[:, tt], ve[:, tt], cst[:, C_HALF:C_HALF + 2], ALU.pow).then_inc(s_rs, 1)

            pool.wait_ge(p_bd, 5)
            nc.gpsimd.memset(vp[:, :, :, :, :], 0.0).then_inc(s_one, 1)
            rsqrt_ln(0, 0)

            def fill(dst, value):
                src = iota8[:, value:value + 1].broadcast_to(dst.shape)
                return nc.gpsimd.tensor_tensor(dst, src, src, ALU.mult)

            def beside_v(value):
                to = vp[:, :, :, 1:3, :].rearrange("p t n g e -> p (t n) (g e)")
                src = iota8[:, None, value:value + 1].broadcast_to([P, T * H // 2, 2 * DK])
                nc.gpsimd.tensor_tensor(to, src, src, ALU.mult).then_inc(s_one, 1)

            with pool.Fori(0, B) as b:
                for c in range(T):
                    if c >= 2:
                        pool.wait_ge(s_wd, b * 4 + (c - 1))
                    pool.wait_ge(s_me, b * T + (c + 1))
                    nc.gpsimd.tensor_tensor(sc16[:, c % 2, :], ve[:, :], cst[:, C_HALF:C_HALF + H], ALU.pow
                                            ).then_inc(s_sc16, 1)
                rsqrt_ln(b, 1)
                pool.wait_ge(s_pv, b * 8 + 8)
                beside_v(1)
                pool.wait_ge(s_op, b * 4 + 1)
                fill(spread, 0).then_inc(s_pool, 1)
                pool.wait_ge(s_pool, b * 18 + 1)
                for j, even_odd in ((j, even_odd) for j in range(4) for even_odd in range(2)):
                    rows = slice(32 * j, 32 * j + 32)
                    diag = cst[rows, C_DIAG + even_odd * DK:C_DIAG + (even_odd + 1) * DK]
                    c = (16 * j + 1 + 4 * even_odd) * DK
                    diag2 = diag[:, None, :].broadcast_to([32, 2, DK])
                    nc.gpsimd.tensor_tensor(spread[rows, c:c + 2 * DK].rearrange("p (g d) -> p g d", g=2), diag2, diag2,
                                            ALU.mult).then_inc(s_pool, 1)
                    c = (16 * j + 9 + 4 * even_odd) * DK
                    nc.gpsimd.tensor_tensor(spread[rows, c:c + DK], diag, diag, ALU.mult).then_inc(s_pool, 1)
                pool.wait_ge(s_pool, b * 18 + 17)
                rsqrt_ln(b, 2)
                pool.wait_ge(s_dn, b * (2 * FT) + FT)
                fill(kflat[:, 0:L], 0).then_inc(s_pool, 1)
                pool.wait_ge(s_tok, b * (4 * TS) + 12)
                for t in range(T):
                    i = nc.gpsimd.tensor_tensor(x[:, t, :], x[:, t, :], rowb[:, 1, :], ALU.add)
                i.then_inc(s_xb, 1)
                pool.wait_ge(s_pvb, b * (NT * NJ) + NT * NJ)
                beside_v(0)
                rsqrt_ln(b, 3)
                rsqrt_ln(b, 4)

        @block.scalar
        def _(act):
            def split_hi(b, i):
                for k in range(KD):
                    act.wait_ge(s_tr, b * (2 * TS - 2) + (2 * (i - (i > 3)) + k + 1))
                    nc.scalar.copy(xt[:, 0, k, :], bank[:, TURNED[i][k], :]).then_inc(s_hi, 1)

            def high_part(i):
                _, hi, _, _, factor = pieces[i]
                piece_in(act, i)
                if factor is None:
                    nc.scalar.copy(hi, staged(i)).then_inc(w_hi, 1)
                else:
                    nc.scalar.activation(hi, staged(i), ACT.Copy, scale=vec[:, factor:factor + 1]).then_inc(w_hi, 1)

            act.wait_ge(l_wa, 48)
            for i in range(FIRST):
                high_part(i)
            for w in range(4):
                act.wait_ge(p_fold, w + 1)
                nc.scalar.copy(w_feat[:, 0, w, :, :], bank[:, w, :].rearrange("p (k n) -> p k n", k=KD)).then_inc(p_fhi, 1)
            for i in range(FIRST, TURN):
                high_part(i)
            split_hi(0, 0)
            for i in range(TURN, NPC):
                high_part(i)
            act.wait_ge(w_lo, NPC)

            with act.Fori(0, B) as b:

                def split_qk_hi(n, half, is_q):
                    act.wait_ge(s_qk, b * 8 + n)
                    if not is_q:
                        nc.scalar.copy(ks[:, 0, half, :], qk[:, half, :]).then_inc(s_sph, 1)
                    else:
                        for odd in range(2):
                            nc.scalar.activation(qs[:, 0, half, odd, :], qk[:, 2 + half, :], ACT.Copy,
                                                 scale=cst[:, C_EVEN + odd:C_EVEN + odd + 1]).then_inc(s_sph, 1)

                def widen(c):
                    act.wait_ge(s_sc16, b * 4 + (c + 1))
                    if c == 0:
                        act.wait_ge(s_out, b * 16 + 16)
                    if c >= 2:
                        act.wait_ge(s_bc, b * 4 + (c - 1))
                    nc.scalar.copy(wide_at(c).rearrange("p (h d) -> p h d", d=DK),
                                   sc16[:, c % 2, :, None].broadcast_to([P, H, DK])).then_inc(s_wd, 1)

                def high_out(c):
                    act.wait_ge(s_on, b * 4 + (c + 1))
                    cols = slice(c * P, (c + 1) * P)
                    nc.scalar.copy(xt[:, 0, :, cols], on[:, :, cols]).then_inc(s_onh, 1)

                for j in range(4):
                    act.wait_ge(s_pj, b * 4 + (j + 1))
                    if j >= 2:
                        act.wait_ge(s_qk, b * 8 + (j - 1))
                    nc.scalar.activation(work[:, j % 2, :], bank[:, (2 * j + 2) % 8, :], ACT.Identity,
                                         bias=vec[:, (V_Q1, V_Q1, V_K1, V_K1)[j]:(V_Q1, V_Q1, V_K1, V_K1)[j] + 1]
                                         ).then_inc(s_tmp, 1)
                    if j >= 1:
                        split_qk_hi(j, (j - 1) % 2, j - 1 < 2)
                split_qk_hi(4, 1, False)
                for t in range(T):
                    act.wait_ge(s_vp, b * 4 + (t // 2 + 1))
                    nc.scalar.copy(v_at(t, 0, H), bank[:, 2 + t // 2, (t % 2) * D:(t % 2 + 1) * D].rearrange(
                        "p (n a e) -> p n a e", a=2, e=DK)).then_inc(s_vs, 1)
                for i in range(2):
                    act.wait_ge(s_kt, b * 2 + (i + 1))
                    nc.scalar.copy(ktok[:, :, i * P:(i + 1) * P], bank[:, 4 + i, :].rearrange("p (t n) -> p t n", t=T)
                                   ).then_inc(s_ktok, 1)
                for c in range(T):
                    act.wait_ge(s_oc, b * 4 + (c + 1))
                    if c:
                        act.wait_ge(s_qm, b * T + c)
                    nc.scalar.activation(sq.rearrange("p (k l) -> p k l", k=KD), on[:, :, c * P:(c + 1) * P], ACT.Square
                                         ).then_inc(s_sq, 1)
                    if c >= 1:
                        widen(c - 1)
                    if c >= 2:
                        high_out(c - 2)
                widen(T - 1)
                high_out(T - 2)
                high_out(T - 1)

                def ffn(f):
                    split_hi(b, 1 if f == 0 else 4)

                    def high(i):
                        act.wait_ge(s_h, b * (2 * FT) + (f * FT + i + 1))
                        if i >= 3:
                            act.wait_ge(s_dn, b * (2 * FT) + (f * FT + i - 2))
                        nc.scalar.copy(hs[:, 2 * (i % 3), :], work[:, 3 + i % 2, :]).then_inc(s_hh, 1)

                    for i in range(FT):
                        act.wait_ge(s_up, b * (2 * FT) + (f * FT + i + 1))
                        if i == 0:
                            nc.scalar.copy(logits, bank[:, 4, :]).then_inc(s_lc, 1)
                        nc.scalar.activation(work[:, i % 2, :], bank[:, 4 + i % 2, :], ACT.Silu).then_inc(s_sg, 1)
                        if i >= 1:
                            high(i - 1)
                        if i == 1:
                            act.wait_ge(s_gv, b * (2 * GV) + (f * GV + 2))
                            nc.scalar.activation(gb[:, :, :], ga[:, :, :], ACT.Exp).then_inc(s_ge, 1)
                    high(FT - 1)
                    if f == 1:
                        split_hi(b, 5)

                ffn(0)
                split_hi(b, 2)

                def half_high(half):
                    for op in range(2):
                        act.wait_ge(s_qk, b * 8 + (4 + 2 * half + op + 1))
                        nc.scalar.copy(ks[:, 0, op, :], qk[:, 2 * op + half, :]).then_inc(s_bh, 1)

                def stack_out(tau, op):
                    k = RING_AT["stack", tau, op]
                    act.wait_ge(s_x, b * NR + (k + 1))
                    if op == 0:
                        nc.scalar.activation(stack[:, tau % 3, 0, :], bank[:, k % 3, :], ACT.Identity,
                                             bias=cst[:, C_ONE:C_ONE + 1]).then_inc(s_xa, 1)
                    else:
                        nc.scalar.copy(stack[:, tau % 3, 1, :], bank[:, k % 3, :]).then_inc(s_xa, 1)

                def exponentials(tau, y):
                    act.wait_ge(s_k, b * (NT * NJ) + (tau * NJ + y + 1))
                    if tau:
                        act.wait_ge(s_pvb, b * (NT * NJ) + ((tau - 1) * NJ + y + 1))
                    at, c, n = slot(y)
                    nc.scalar.activation(probs[:, at, c:c + n], bank[:, 3 + (tau * NJ + y) % 4, 0:n], ACT.Exp,
                                         scale=DK ** -0.5).then_inc(s_e, 1)

                def raw_out(r):
                    act.wait_ge(s_pvb, b * (NT * NJ) + (2 * r + 2) * NJ)
                    if r >= 2:
                        act.wait_ge(s_tok, b * (4 * TS) + (12 + r - 1))
                    nc.scalar.copy(raw[:, r % 2, :], bank[:, 7, :]).then_inc(s_u, 1)

                def turned_high(half):
                    k = RING_AT["half", half]
                    act.wait_ge(s_x, b * NR + (k + 1))
                    nc.scalar.copy(xt[:, 0, half, :], bank[:, k % 3, :]).then_inc(s_hi, 1)

                half_high(0)
                for tau in range(-3, NT):
                    if tau >= 0:
                        for y in (4, 5):
                            exponentials(tau, y)
                    if tau + 3 < NT:
                        for op in range(2):
                            stack_out(tau + 3, op)
                    if tau == 0:
                        half_high(1)
                    if tau == HALF_DONE[0]:
                        turned_high(0)
                    if 0 <= tau + 1 < NT:
                        for y in range(4):
                            exponentials(tau + 1, y)
                    if tau >= 0 and tau % 2 == 1 and tau < NT - 1:
                        raw_out(tau // 2)
                raw_out(NT // 2 - 1)
                turned_high(1)
                ffn(1)

        @block.vector
        def _(dve):
            dve.wait_ge(l_cst, 48)
            nc.vector.tensor_copy(ident16[:, :], ident).then_inc(p_c16, 1)
            nc.vector.tensor_scalar(neg16[:, :], tri, 1.0, -NEG, ALU.subtract, ALU.mult).then_inc(p_c16, 1)
            nc.vector.tensor_copy(sel16[:, 0:sel_a], sel_raw[0]).then_inc(p_c16, 1)
            nc.vector.tensor_copy(sel16[:, sel_a:sel_n], sel_raw[1]).then_inc(p_c16, 1)
            nc.vector.memset(c16[:, :, 3 * E:32], 0.0).then_inc(p_c16, 1)
            dve.wait_ge(l_wa, 48)
            for w in range(4):
                src = fm[:, w, None, :].broadcast_to([P, P // DK, DK])
                nc.vector.scalar_tensor_tensor(bd[:, w, :].rearrange("p (h d) -> p h d", d=DK), src, DK ** -0.5 if w == 0 else 1.0,
                                               bdmask.rearrange("p (h d) -> p h d", d=DK), ALU.mult, ALU.mult
                                               ).then_inc(p_bd, 1)
            nc.vector.tensor_scalar(vec[:, V_Q1:V_Q1 + 1], vec[:, V_Q1:V_Q1 + 1], DK ** -0.5, None, ALU.mult).then_inc(p_bd, 1)
            carried = [0]

            def carry(semaphore, value):
                dve.wait_ge(semaphore, value)
                nc.vector.tensor_copy(spare[:, carried[0]:carried[0] + 1], cst[:, C_ODD:C_ODD + 1])
                carried[0] += 1

            def statistics(b, s, h, src):
                tiles = (2 * h, 2 * h + 1)
                for t in tiles:
                    nc.vector.bn_stats(st6[:, t, :], src[:, t, :]).then_inc(s_bn, 1)
                if isinstance(b, int):
                    dve.wait_ge(s_bn, 2 * h + 2)
                else:
                    carry(s_bn, b * 16 + (4 * s + 2 * h + 2))
                for t in tiles:
                    nc.vector.bn_aggr(mv[:, t, :], st6[:, t, :]).then_inc(s_ag, 1)
                dve.wait_ge(s_ag, b * 16 + (4 * s + 2 * h + 2))
                nc.vector.tensor_scalar(ve[:, 2 * h:2 * h + 2], mv[:, 2 * h:2 * h + 2, 1], EPS, None, ALU.add).then_inc(s_ve, 1)

            def normalized(b, s, src):
                for t in range(T):
                    if t % 2 == 0:
                        dve.wait_ge(s_rs, b * 8 + (2 * s + t // 2 + 1))
                    nc.vector.tensor_scalar(xn[:, t, :], src[:, t, :], mv[:, t, 0:1], rstd[:, t:t + 1],
                                            ALU.subtract, ALU.mult).then_inc(s_tok, 1)

            def split_lo(b, i):
                for k in range(KD):
                    dve.wait_ge(s_hi, b * (2 * TS) + (2 * i + k + 1))
                    nc.vector.tensor_tensor(xt[:, 1, k, :], bank[:, TURNED[i][k], :], xt[:, 0, k, :].bitcast(F32),
                                            ALU.subtract).then_inc(s_lo, 1)

            def low_part(i):
                _, hi, lo, _, factor = pieces[i]
                dve.wait_ge(w_hi, i + 1)
                if factor is None:
                    nc.vector.tensor_tensor(lo, staged(i), hi.bitcast(F32), ALU.subtract).then_inc(w_lo, 1)
                else:
                    nc.vector.scalar_tensor_tensor(lo, staged(i), vec[:, factor:factor + 1], hi.bitcast(F32),
                                                   ALU.mult, ALU.subtract).then_inc(w_lo, 1)

            for i in range(FIRST):
                low_part(i)
            for w in range(4):
                dve.wait_ge(p_fhi, w + 1)
                nc.vector.tensor_tensor(w_feat[:, 1, w, :, :], bank[:, w, :].rearrange("p (k n) -> p k n", k=KD),
                                        w_feat[:, 0, w, :, :].bitcast(F32), ALU.subtract).then_inc(p_flo, 1)
            dve.wait_ge(l_x, 16)
            for h in range(2):
                statistics(0, 0, h, xin)
            for i in range(FIRST, TURN):
                low_part(i)
            normalized(0, 0, xin)
            split_lo(0, 0)
            for i in range(TURN, NPC):
                low_part(i)
            dve.wait_ge(w_lo, NPC)
            dve.wait_ge(p_c16, 5)
            dve.wait_ge(s_one, 1)

            with dve.Fori(0, B) as b:
                def split_qk_lo(n, half, is_q):
                    dve.wait_ge(s_sph, b * 6 + n)
                    if not is_q:
                        nc.vector.tensor_tensor(ks[:, 1, half, :], qk[:, half, :], ks[:, 0, half, :].bitcast(F32),
                                                ALU.subtract).then_inc(s_spl, 1)
                    else:
                        for odd in range(2):
                            nc.vector.scalar_tensor_tensor(qs[:, 1, half, odd, :], qk[:, 2 + half, :],
                                                           cst[:, C_EVEN + odd:C_EVEN + odd + 1],
                                                           qs[:, 0, half, odd, :].bitcast(F32),
                                                           ALU.mult, ALU.subtract).then_inc(s_spl, 1)

                def outputs_raw(c):
                    dve.wait_ge(s_pv, b * 8 + 2 * (c + 1))
                    nc.vector.tensor_copy(on[:, :, c * P:(c + 1) * P],
                                          bank[:, 4 + c % 2, 0:D].rearrange("p (k l) -> p k l", k=KD)).then_inc(s_oc, 1)

                def scaled(c):
                    dve.wait_ge(s_bc, b * 4 + (c + 1))
                    dve.wait_ge(s_oc, b * 4 + (c + 1))
                    nc.vector.tensor_tensor(on[:, :, c * P:(c + 1) * P], on[:, :, c * P:(c + 1) * P],
                                            bank[:, 6 + c % 2, D:2 * D].rearrange("p (k l) -> p k l", k=KD), ALU.mult
                                            ).then_inc(s_on, 1)

                def low_out(c):
                    dve.wait_ge(s_onh, b * 4 + (c + 1))
                    cols = slice(c * P, (c + 1) * P)
                    nc.vector.tensor_tensor(xt[:, 1, :, cols], on[:, :, cols], xt[:, 0, :, cols].bitcast(F32),
                                            ALU.subtract).then_inc(s_onl, 1)

                def residual(n, first, base, before=(), then=None, between=lambda: None):
                    for i in range(2):
                        if before:
                            dve.wait_ge(*before[i])
                        nc.vector.tensor_tensor(x[:, 2 * i:2 * i + 2, :], base[:, 2 * i:2 * i + 2, :],
                                                bank[:, first + i, :].rearrange("p (t n) -> p t n", t=2),
                                                ALU.add).then_inc(s_res, 1)
                        dve.wait_ge(s_res, b * 8 + (2 * n + i + 1))
                        if then is not None:
                            statistics(b, then, i, x)
                        if i == 0:
                            between()
                    if then is not None:
                        normalized(b, then, x)

                for j in range(4):
                    dve.wait_ge(s_tmp, b * 4 + (j + 1))
                    v2 = (V_Q2, V_Q2, V_K2, V_K2)[j]
                    nc.vector.scalar_tensor_tensor(qk[:, (j + 2) % 4, :], bank[:, (2 * j + 3) % 8, :], vec[:, v2:v2 + 1],
                                                   work[:, j % 2, :], ALU.add, ALU.mult).then_inc(s_qk, 1)
                    if j in (1, 2):
                        split_qk_lo(2 * j, j - 1, True)
                for half in range(KD):
                    split_qk_lo(5 + half, half, False)

                def scores_out(m):
                    dve.wait_ge(s_sc, b * 8 + (m + 1))
                    if m >= 2:
                        dve.wait_ge(s_pv, b * 8 + (m - 1))
                    for i in range(2):
                        nc.vector.tensor_tensor(work[:, 2 * (m % 2) + i, :].rearrange("p (h c) -> p h c", h=4),
                                                bank[:, 2 * (m % 2) + i, :].rearrange("p (h c) -> p h c", h=4),
                                                tri[:, None, :].broadcast_to([P, 4, P]), ALU.mult).then_inc(s_st, 1)

                def states_out():
                    for i, (lo, hi) in enumerate(((0, 2), (2, 3))):
                        dve.wait_ge(s_kv, b * 2 + (i + 1))
                        n = 2 * (hi - lo)
                        nc.vector.tensor_tensor(kvm[:, lo:hi, :].rearrange("p a (h n) -> p (a h) n", n=P),
                                                bank[:, 6 + i, 0:n * P].rearrange("p (a n) -> p a n", n=P),
                                                bdmask[:, None, :].broadcast_to([P, n, P]), ALU.mult).then_inc(s_kvm, 1)

                def mean_squares(c):
                    dve.wait_ge(s_qm, b * T + (c + 1))
                    if c:
                        dve.wait_ge(s_sc16, b * 4 + c)
                    nc.vector.tensor_scalar(ve[:, :], bank[:, 6 + c % 2, 0:H], 1.0 / DK, EPS, ALU.mult, ALU.add
                                            ).then_inc(s_me, 1)

                states_out()
                scores_out(0)
                for m in range(1, 8):
                    scores_out(m)
                    if m >= 3 and m % 2 == 1:
                        outputs_raw((m - 3) // 2)
                    if m >= 4 and m % 2 == 0:
                        mean_squares(m // 2 - 2)
                scaled(0)
                low_out(0)
                mean_squares(2)
                scaled(1)
                outputs_raw(3)
                mean_squares(3)
                low_out(1)
                scaled(2)
                low_out(2)
                dve.wait_ge(s_out, b * 16 + 16)

                def last_chunk():
                    scaled(3)
                    low_out(3)

                residual(0, 2, xin, [(s_op, b * 4 + 1), (s_op, b * 4 + 2)], 1, last_chunk)

                def ffn(f):
                    i0 = 1 if f == 0 else 4
                    split_lo(b, i0)
                    g = [f * GV]

                    def step(ins, wait=True):
                        g[0] += 1
                        ins.then_inc(s_gv, 1)
                        if wait:
                            dve.wait_ge(s_gv, b * (2 * GV) + g[0])

                    def wide(a):
                        return a.broadcast_to([P, T, E])

                    def routing():
                        dve.wait_ge(s_lg, b * 2 + (f + 1))
                        lg = bank[:, 2, :].rearrange("p (t e) -> p t e", e=P)[:, :, 0:E]
                        step(nc.vector.tensor_reduce(gs[:, 0, :], lg, AX_X, ALU.max))
                        step(nc.vector.tensor_tensor(ga[:, :, :], lg, wide(gs[:, 0, :, None]), ALU.subtract), False)
                        dve.wait_ge(s_ge, b * 2 + (f + 1))
                        step(nc.vector.tensor_reduce(gs[:, 1, :], gb[:, :, :], AX_X, ALU.add))
                        step(nc.vector.reciprocal(gs[:, 2, :], gs[:, 1, :]))
                        step(nc.vector.tensor_tensor(ga[:, :, :], gb[:, :, :], wide(gs[:, 2, :, None]), ALU.mult), False)
                        carry(s_gv, b * (2 * GV) + g[0])
                        for t in range(T):
                            ins = nc.vector.max(gtop[:, t, :], ga[:, t, :])
                        step(ins, False)
                        carry(s_gv, b * (2 * GV) + g[0])
                        for t in range(T):
                            ins = nc.vector.max_index(gidx[:, t, :], gtop[:, t, :], ga[:, t, :])
                        step(ins)
                        step(nc.vector.tensor_copy(gidf[:, :, :], gidx[:, :, 0:2]), False)
                        step(nc.vector.scalar_tensor_tensor(gs[:, 3, :], gtop[:, :, 0], 1e-20, gtop[:, :, 1], ALU.add, ALU.add))
                        step(nc.vector.reciprocal(gs[:, 1, :], gs[:, 3, :]))
                        for j in range(2):
                            nc.vector.tensor_tensor(gw[:, j, :], gtop[:, :, j], gs[:, 1, :], ALU.mult)
                            ins = nc.vector.tensor_tensor(geq[:, j, :, :], iota8[:, None, :].broadcast_to([P, T, E]),
                                                          wide(gidf[:, :, j:j + 1]), ALU.is_equal)
                        step(ins)
                        for j in range(2):
                            ins = nc.vector.tensor_tensor(cmb[:, j, :, :], geq[:, j, :, :], wide(gw[:, j, :, None]), ALU.mult)
                        step(ins)
                        step(nc.vector.tensor_tensor(ga[:, :, :], cmb[:, 0, :, :], cmb[:, 1, :, :], ALU.add))
                        step(nc.vector.tensor_copy(c16[:, :, 0:E], ga[:, :, :]))
                        step(nc.vector.tensor_tensor(cmb[:, 2, :, :], ga[:, :, :], c16[:, :, 0:E], ALU.subtract))
                        step(nc.vector.tensor_copy(c16[:, :, E:2 * E], cmb[:, 2, :, :]))
                        assert g[0] == f * GV + GV
                        nc.vector.tensor_tensor(c16[:, :, 2 * E:3 * E], cmb[:, 2, :, :], c16[:, :, E:2 * E],
                                                ALU.subtract).then_inc(s_c16, 1)

                    def n(i):
                        return b * (2 * FT) + (f * FT + i + 1)

                    def low(i):
                        dve.wait_ge(s_hh, n(i))
                        nc.vector.tensor_tensor(hs[:, 2 * (i % 3) + 1, :], work[:, 3 + i % 2, :],
                                                hs[:, 2 * (i % 3), :].bitcast(F32), ALU.subtract).then_inc(s_hl, 1)

                    for i in range(FT):
                        if i == SHARED_TILES:
                            dve.wait_ge(s_ctp, b * 2 + (f + 1))
                            nc.vector.tensor_copy(ct16, bank[0:32, 2, 0:256].bitcast(BF16)).then_inc(s_ct, 1)
                        dve.wait_ge(s_sg, n(i))
                        if i < SHARED_TILES:
                            nc.vector.tensor_tensor(work[:, 3 + i % 2, :], bank[:, 6 + i % 2, :], work[:, i % 2, :],
                                                    ALU.mult).then_inc(s_h, 1)
                        else:
                            if i > SHARED_TILES:
                                dve.wait_ge(s_h, n(i - 1))
                            nc.vector.tensor_tensor(work[:, 2, :], bank[:, 6 + i % 2, :], work[:, i % 2, :],
                                                    ALU.mult).then_inc(s_t1, 1)
                            dve.wait_ge(s_t1, b * (2 * (FT - SHARED_TILES)) + (f * (FT - SHARED_TILES) + i - SHARED_TILES + 1))
                            nc.vector.tensor_tensor(work[:, 3 + i % 2, :], bank[:, 2 + i % 2, :], work[:, 2, :],
                                                    ALU.mult).then_inc(s_h, 1)
                        if i >= 1:
                            low(i - 1)
                        if i == 1:
                            routing()
                        if f == 1 and i in (6, 7):
                            if i == 6:
                                dve.wait_ge(l_x, b * 16 + 32)
                            statistics(b, 4, i - 6, xin)
                        if f == 1 and i == 9:
                            normalized(b, 4, xin)
                    low(FT - 1)
                    if f == 1:
                        split_lo(b, 5)

                def products_done(f):
                    return [(s_dh, b * 2 + (f + 1)), (s_dn, b * (2 * FT) + (f + 1) * FT)]

                ffn(0)
                residual(1, 0, x, products_done(0), 2)

                split_lo(b, 2)

                def half_low(half):
                    for op in range(2):
                        dve.wait_ge(s_bh, b * 4 + (2 * half + op + 1))
                        nc.vector.tensor_tensor(ks[:, 1, op, :], qk[:, 2 * op + half, :],
                                                ks[:, 0, op, :].bitcast(F32), ALU.subtract).then_inc(s_bl, 1)

                def qk_out(half, op):
                    n = 2 * half + op
                    dve.wait_ge(s_bp, b * 4 + (n + 1))
                    c = (V_BK, V_BQ)[op] + half
                    nc.vector.scalar_tensor_tensor(qk[:, 2 * op + half, :], bank[:, 2 + n, :], vec[:, c:c + 1],
                                                   emb, ALU.add, ALU.mult).then_inc(s_qk, 1)

                def v_out(i):
                    dve.wait_ge(s_vp, b * 4 + (2 + i + 1))
                    for t in (2 * i, 2 * i + 1):
                        nc.vector.tensor_tensor(v_at(t, 0, H), bank[:, 6 + i, (t % 2) * D:(t % 2 + 1) * D].rearrange(
                            "p (n a e) -> p n a e", a=2, e=DK), rowb[:, 0, :].rearrange("p (n a e) -> p n a e", a=2, e=DK),
                                                ALU.add).then_inc(s_vs, 1)

                for op in range(2):
                    qk_out(0, op)
                half_low(0)
                v_out(0)

                def shift_out(tau, src):
                    nc.vector.tensor_tensor(stack[:, tau % 3, 1, :], stack[:, tau % 3, 1, :].bitcast(F32), src,
                                            ALU.add).then_inc(s_xf, 1)

                def maxima(tau, n, src):
                    if n == 0 and tau:
                        dve.wait_ge(s_sh, b * (2 * NT) + 2 * tau)
                    if n < 2:
                        nc.vector.tensor_reduce(mx[:, n, 3:4], src, AX_X, ALU.max).then_inc(s_xf, 1)
                    elif n < 4:
                        nc.vector.tensor_reduce(mx[:, n - 2, 2:3], src[:, 0:3 * P], AX_X, ALU.max).then_inc(s_mx, 1)
                        nc.vector.tensor_reduce(mx[:, n - 2, 0:1], src[:, 3 * P:4 * P], AX_X, ALU.max).then_inc(s_xf, 1)
                    else:
                        nc.vector.tensor_reduce(mx[:, n - 4, 1:2], src[:, 0:2 * P], AX_X, ALU.max).then_inc(s_xf, 1)
                    if n == NJ - 1:
                        dve.wait_ge(s_xf, b * (NR - NSTACK) + ring_read(("scores", tau, n))[1])
                        dve.wait_ge(s_mx, b * (2 * NT) + 2 * (tau + 1))
                        at = shifts.rearrange("p t (a c) -> p a t c", a=2)
                        nc.vector.tensor_scalar(at[:, :, :, SHIFT].bitcast(F32R), mx[:, :, :], -1.0, None, ALU.mult
                                                ).then_inc(s_sh, 1)
                        dve.wait_ge(s_sh, b * (2 * NT) + (2 * tau + 1))
                        nc.vector.scalar_tensor_tensor(at[:, :, :, SHIFT + 1].bitcast(F32R), mx[:, :, :], -1.0,
                                                       at[:, :, :, SHIFT], ALU.mult, ALU.subtract).then_inc(s_sh, 1)

                def outputs_out(r, src):
                    pairs = src.rearrange("p (t n g e) -> p t n g e", t=T, n=2, e=DK)
                    inv = ve[:, :].rearrange("p (t n a) -> p t n a", t=T, n=2)
                    if r:
                        dve.wait_ge(s_xf, b * (NR - NSTACK) + ring_read(("outputs", r - 1))[1])
                        dve.wait_ge(s_tok, b * (4 * TS) + (12 + r))
                    for a in range(2):
                        ins = nc.vector.reciprocal(inv[:, :, :, a], pairs[:, :, :, 1 + a, 0])
                        ins.then_inc(s_rc, 1)
                    dve.wait_ge(s_rc, b * NT + 2 * (r + 1))
                    to = xn[:, :, 4 * DK * r:4 * DK * (r + 1)].rearrange("p t (n a e) -> p t n a e", a=2, e=DK)
                    for a in range(2):
                        ins = nc.vector.tensor_tensor(to[:, :, :, a, :], pairs[:, :, :, 3 * a, :],
                                                      inv[:, :, :, a, None].broadcast_to([P, T, 2, DK]), ALU.mult)
                        ins.then_inc((s_tok, s_xf)[a], 1)

                def turned_low(half, src):
                    dve.wait_ge(s_hi, b * (2 * TS) + (6 + half + 1))
                    for i in range(2):
                        cols = slice(i * L // 2, (i + 1) * L // 2)
                        ins = nc.vector.tensor_tensor(xt[:, 1, half, cols], src[:, cols], xt[:, 0, half, cols].bitcast(F32),
                                                      ALU.subtract)
                        ins.then_inc((s_lo, s_xf)[i], 1)

                for tau in range(-3, NT + 1):
                    for job in RING[tau]:
                        if job[0] == "stack":
                            continue
                        k = RING_AT[job]
                        src = bank[:, k % 3, :]
                        dve.wait_ge(s_x, b * NR + (k + 1))
                        if job[0] == "shift":
                            shift_out(job[1], src)
                        elif job[0] == "scores":
                            maxima(job[1], job[2], src)
                            if tau == -2 and job[2] == 3:
                                for op in range(2):
                                    qk_out(1, op)
                        elif job[0] == "half":
                            turned_low(job[1], src)
                        else:
                            outputs_out(job[1], src)
                    if tau == -3:
                        v_out(1)
                    if tau == 0:
                        half_low(1)
                dve.wait_ge(s_xb, b + 1)
                residual(2, 5, x, [(s_op, b * 4 + 3), (s_op, b * 4 + 4)], 3)
                ffn(1)
                residual(3, 0, x, products_done(1))

        @block.tensor
        def _(pe):
            pe.wait_ge(l_cst, 48)
            for w in range(4):
                pe.wait_ge(p_bd, w + 1)
                for k in range(KD):
                    for half in range(KD):
                        ins = nc.tensor.matmul(bank[:, w, (2 * k + half) * P:(2 * k + half + 1) * P],
                                               wqk_raw[:, w // 2, half, k * P:(k + 1) * P], bd[:, w, :],
                                               start=True, stop=True)
                ins.then_inc(p_fold, 1)
            def transposed(b, i):
                for t in range(T):
                    pe.wait_ge(s_tok, b * (4 * TS) + (4 * i + t + 1))
                    for k in range(KD):
                        ins = nc.tensor.matmul(bank[:, TURNED[i][k], t * P:(t + 1) * P], xn[:, t, k * P:(k + 1) * P], ident,
                                               start=True, stop=True, is_transpose=True)
                        if t == T - 1:
                            ins.then_inc(s_tr, 1)

            transposed(0, 0)
            pe.wait_ge(p_flo, 4)

            with pe.Fori(0, B) as b:
                PASSES = ((0, 0), (1, 0), (0, 1))

                def by_feature(dst, weight, i=None):
                    for n, (k, (a, c)) in enumerate((k, ac) for k in range(KD) for ac in PASSES):
                        if i is not None and n % 3 == 0:
                            pe.wait_ge(s_hi, b * (2 * TS) + (2 * i + k + 1))
                        if i is not None and n % 3 == 2:
                            pe.wait_ge(s_lo, b * (2 * TS) + (2 * i + k + 1))
                        ins = nc.tensor.matmul(dst, weight(a, k), xt[:, c, k, :], start=(n == 0), stop=(n == 3 * KD - 1))
                    return ins

                def by_token(dst, t, weight, first):
                    for n, (k, (a, c)) in enumerate((k, ac) for k in range(KD) for ac in PASSES):
                        ins = nc.tensor.matmul(dst, xt[:, a, k, t * P:(t + 1) * P], weight(c, k),
                                               start=(first and n == 0), stop=(n == 3 * KD - 1), skip_group_check=True)
                    return ins

                def two_banks(first, weight, done, before=lambda t: None):
                    for t in range(T):
                        before(t)
                        ins = by_token(bank[:, first + t // 2, (t % 2) * D:(t % 2 + 1) * D], t, weight, t % 2 == 0)
                        if t % 2:
                            ins.then_inc(done, 1)

                for j in range(4):
                    half, pair = j % 2, (0, 0, 2, 2)[j]
                    if j == 3:
                        pe.wait_ge(s_res, b * 8)
                    for i in range(2):
                        ins = by_feature(bank[:, (2 * j + 2 + i) % 8, :],
                                         lambda a, k: w_feat[:, a, pair + i, k, half * P:(half + 1) * P],
                                         0 if (i, j) == (0, 0) else None)
                    ins.then_inc(s_pj, 1)
                pe.wait_ge(s_qk, b * 8 + 1)
                pe.wait_ge(w_lo, 2)
                two_banks(2, lambda c, k: w_v[:, c, k, :], s_vp)
                for half in range(KD):
                    pe.wait_ge(s_qk, b * 8 + 4)
                    for t in range(T):
                        ins = nc.tensor.matmul(bank[:, 4 + half, t * P:(t + 1) * P], qk[:, half, t * P:(t + 1) * P],
                                               ident, start=True, stop=True, is_transpose=True)
                    ins.then_inc(s_kt, 1)

                def scores(m):
                    c = m // 2
                    if m >= 2:
                        pe.wait_ge(s_st, b * 16 + 2 * (m - 1))
                    cols = slice(c * P, (c + 1) * P)
                    for half in range(KD):
                        for n, (a, q) in enumerate(PASSES):
                            for i in range(2):
                                rows = slice(32 * (2 * (m % 2) + i), 32 * (2 * (m % 2) + i) + 32)
                                ins = nc.tensor.matmul(bank[:, 2 * (m % 2) + i, half * 2 * P:(half + 1) * 2 * P],
                                                       ks[rows, a, half, cols], qs[rows, q, half, :, cols],
                                                       start=(n == 0), stop=(n == 2))
                    ins.then_inc(s_sc, 1)

                def states():
                    pe.wait_ge(s_ktok, b * 2 + 2)
                    pe.wait_ge(s_vs, b * (2 * T) + T)
                    for n in range(1, T):
                        for half in range(KD):
                            cols = slice(half * P, (half + 1) * P)
                            at = ((n - 1) % 2) * D + half * P
                            for c in range(n):
                                ins = nc.tensor.matmul(bank[:, 6 + (n - 1) // 2, at:at + P], ktok[:, c, cols],
                                                       v_at(c, 8 * half, 8 * half + 8), start=(c == 0), stop=(c == n - 1))
                        if n >= 2:
                            ins.then_inc(s_kv, 1)

                def products(m):
                    c, o = m // 2, 4 + m // 2 % 2
                    if m % 2 == 0:
                        if c == 1:
                            pe.wait_ge(s_kvm, b * 2 + 2)
                        if c >= 2:
                            pe.wait_ge(s_oc, b * 4 + (c - 1))
                        if c:
                            for half in range(KD):
                                cols = slice(half * P, (half + 1) * P)
                                nc.tensor.matmul(bank[:, o, cols], kvm[:, c - 1, cols], qk[:, 2 + half, c * P:(c + 1) * P],
                                                 start=(half == 0), stop=False, skip_group_check=True)
                    pe.wait_ge(s_st, b * 16 + 2 * (m + 1))
                    for hp in range(4):
                        half, odd = hp // 2, hp % 2
                        for i in range(2):
                            r = 2 * (m % 2) + i
                            ins = nc.tensor.matmul(bank[32 * r:32 * r + 32, o, half * P:(half + 1) * P],
                                                   vp[:, c, half * 4 + r, 2 * odd:2 * odd + 2, :],
                                                   work[:, r, hp * P:(hp + 1) * P],
                                                   start=(c == 0 and odd == 0), stop=(odd == 1), skip_group_check=True,
                                                   tile_position=(0, 32 * r))
                    ins.then_inc(s_pv, 1)

                def squares_summed(c):
                    pe.wait_ge(s_sq, b * T + (c + 1))
                    if c >= 2:
                        pe.wait_ge(s_on, b * 4 + (c - 1))
                    for half in range(KD):
                        ins = nc.tensor.matmul(bank[:, 6 + c % 2, half * 8:half * 8 + 8], sq[:, half * P:(half + 1) * P],
                                               bdmask[:, 0:P:DK], start=(half == 0), stop=True, skip_group_check=True)
                    ins.then_inc(s_qm, 1)

                def scales_turned(c):
                    pe.wait_ge(s_wd, b * 4 + (c + 1))
                    if c >= 2:
                        pe.wait_ge(s_on, b * 4 + (c - 1))
                    for half in range(KD):
                        ins = nc.tensor.matmul(bank[:, 6 + c % 2, D + half * P:D + (half + 1) * P],
                                               wide_at(c)[:, half * P:(half + 1) * P], ident,
                                               start=True, stop=True, is_transpose=True)
                    ins.then_inc(s_bc, 1)

                pe.wait_ge(s_qk, b * 8 + 4)
                pe.wait_ge(s_one, b * 2 + 1)
                states()
                pe.wait_ge(s_spl, b * 6 + 6)
                scores(0)
                scores(1)
                for m in range(8):
                    products(m)
                    if m + 2 < 8:
                        scores(m + 2)
                    if m >= 2 and m % 2 == 0:
                        squares_summed(m // 2 - 1)
                    if m >= 4 and m % 2 == 0:
                        scales_turned(m // 2 - 2)
                squares_summed(3)
                scales_turned(2)

                def before_output(t):
                    if t == 3:
                        scales_turned(3)
                    pe.wait_ge(s_onl, b * 4 + (t + 1))

                two_banks(2, lambda c, k: w_o[:, c, k, :], s_op, before_output)

                def ffn(f):
                    i0 = 1 if f == 0 else 4
                    transposed(b, i0)
                    pe.wait_ge(w_lo, NPC)
                    pe.wait_ge(p_c16, 5)

                    def n(i):
                        return b * (2 * FT) + (f * FT + i + 1)

                    def up(i):
                        cols = slice(i * P, (i + 1) * P)
                        if i >= 2:
                            pe.wait_ge(s_h, n(i - 2))
                        for g in range(2):
                            ins = by_feature(bank[:, 4 + 2 * g + i % 2, :], lambda a, k: w_gu[:, a, g, k, cols],
                                             i0 if (i, g) == (0, 0) else None)
                        if i == SHARED_TILES:
                            pe.wait_ge(s_c16, b * 2 + (f + 1))
                            for t in range(T):
                                ins = nc.tensor.matmul(bank[0:32, 2, t * 64:(t + 1) * 64].bitcast(BF16), c16[:, t, :],
                                                       ident16[:, :], start=True, stop=True, is_transpose=True)
                            ins.then_inc(s_ctp, 1)
                            pe.wait_ge(s_ct, b * 2 + (f + 1))
                        if i >= SHARED_TILES:
                            ins = nc.tensor.matmul(bank[:, 2 + i % 2, :], sel16[:, i * P - SHARED:(i + 1) * P - SHARED],
                                                   ct16, start=True, stop=True)
                        ins.then_inc(s_up, 1)

                    def down(i):
                        pe.wait_ge(s_hl, n(i))
                        s = 2 * (i % 3)
                        for t in range(T):
                            for a, c in PASSES:
                                ins = nc.tensor.matmul(bank[:, t // 2, (t % 2) * D:(t % 2 + 1) * D],
                                                       hs[:, s + a, t * P:(t + 1) * P], w_dn[:, c, i, :],
                                                       start=(i == 0 and t % 2 == 0 and a == 0 and c == 0),
                                                       stop=(i == FT - 1), skip_group_check=True)
                            if i == FT - 1 and t == 1:
                                ins.then_inc(s_dh, 1)
                        ins.then_inc(s_dn, 1)

                    for i in range(FT + 2):
                        if i < FT:
                            up(i)
                        if i == 1:
                            pe.wait_ge(s_lc, b * 2 + (f + 1))
                            for t in range(T):
                                ins = nc.tensor.matmul(bank[:, 2, t * P:(t + 1) * P], logits[:, t * P:(t + 1) * P],
                                                       ident, start=True, stop=True, is_transpose=True)
                            ins.then_inc(s_lg, 1)
                        if f == 1 and i == FT - 1:
                            pe.wait_ge(s_h, n(FT - 2))
                            transposed(b, 5)
                        if i >= 2:
                            down(i - 2)

                ffn(0)

                transposed(b, 2)

                def qk_projected(half, op):
                    cols = slice(((2, 0)[op] + half) * P, ((2, 0)[op] + half + 1) * P)
                    ins = by_feature(bank[:, 2 + 2 * half + op, :], lambda a, k: w_qkv[:, a, k, cols],
                                     2 if half == op == 0 else None)
                    ins.then_inc(s_bp, 1)

                def v_projected(i):
                    for t in (2 * i, 2 * i + 1):
                        ins = by_token(bank[:, 6 + i, (t % 2) * D:(t % 2 + 1) * D], t,
                                       lambda c, k: w_qkv[:, c, k, 2 * D:3 * D], t % 2 == 0)
                    ins.then_inc(s_vp, 1)

                def masks(o, blocks, by_key):
                    c, n = blocks
                    nc.tensor.matmul(bank[:, o, c:c + n * P].rearrange("p (n c) -> p n c", n=n),
                                     (ident16 if by_key else neg16)[:, :],
                                     (neg16 if by_key else ident16)[:, None, :].broadcast_to([P, n, P]), start=True,
                                     stop=False, skip_group_check=True)

                def wait_read(job):
                    by_scalar, count = ring_read(job)
                    if by_scalar:
                        pe.wait_ge(s_xa, b * NSTACK + count)
                    else:
                        pe.wait_ge(s_xf, b * (NR - NSTACK) + count)

                def ring(job):
                    k = RING_AT[job]
                    if k >= 3:
                        wait_read(ORDER[k - 3])
                    return k % 3

                def turned_shifts(tau):
                    o = ring(("shift", tau))
                    pe.wait_ge(s_sh, b * (2 * NT) + 2 * (tau + 1))
                    for t in range(T):
                        ins = nc.tensor.matmul(bank[:, o, t * P:(t + 1) * P], shifts[:, t, :], ident,
                                               start=True, stop=True, is_transpose=True)
                    ins.then_inc(s_x, 1)

                def scores_by_query(tau, n):
                    o = [ring(("scores", tau, n + a)) for a in range(2)]
                    if n == 0:
                        wait_read(("stack", tau, 1))
                    for a in range(2):
                        masks(o[a], diagonals(QUERY_JOBS[n + a], False), False)
                    for i in range(len(QUERY_JOBS[n])):
                        for a in range(2):
                            _, qt, c = QUERY_JOBS[n + a][i]
                            rows = slice(64 * a, 64 * a + 64)
                            ins = nc.tensor.matmul(bank[:, o[a], c:c + (qt + 1) * P],
                                                   stack[rows, tau % 3, 1, qt * P:(qt + 1) * P],
                                                   stack[rows, tau % 3, 0, 0:(qt + 1) * P], start=False, stop=True,
                                                   skip_group_check=True)
                            if i == len(QUERY_JOBS[n]) - 1:
                                ins.then_inc(s_x, 1)

                def stacked(tau, op):
                    o = ring(("stack", tau, op))
                    pe.wait_ge(s_bl, b * 4 + (2 * (tau // 4) + op + 1))
                    if tau == 0 and op == 0:
                        pe.wait_ge(s_pool, b * 18 + 18)
                    high, low = (16 * (tau % 4) + g for g in ((1, 7), (0, 9))[op])
                    nc.tensor.matmul(bank[:, o, :], spread[:, high * DK:high * DK + P], ks[:, 0, op, :],
                                     start=True, stop=False)
                    nc.tensor.matmul(bank[:, o, :], spread[:, low * DK:low * DK + P], ks[:, 1, op, :],
                                     start=False, stop=True).then_inc(s_x, 1)

                def turned_outputs(r):
                    o = ring(("outputs", r))
                    pe.wait_ge(s_u, b * 4 + (r + 1))
                    for t in range(T):
                        ins = nc.tensor.matmul(bank[:, o, t * P:(t + 1) * P], raw[:, r % 2, t * P:(t + 1) * P], ident,
                                               start=True, stop=True, is_transpose=True)
                    ins.then_inc(s_x, 1)

                def turned_half(half):
                    o = ring(("half", half))
                    pe.wait_ge(s_tok, b * (4 * TS) + (12 + 2 * (half + 1)))
                    wait_read(("outputs", 2 * half + 1))
                    for t in range(T):
                        ins = nc.tensor.matmul(bank[:, o, t * P:(t + 1) * P], xn[:, t, half * P:(half + 1) * P], ident,
                                               start=True, stop=True, is_transpose=True)
                    ins.then_inc(s_x, 1)

                def output_projected(half):
                    pe.wait_ge(s_hi, b * (2 * TS) + (6 + half + 1))
                    pe.wait_ge(s_lo, b * (2 * TS) + (6 + half + 1))
                    wait_read(("half", half))
                    for t in range(T):
                        for n, (a, c) in enumerate(PASSES):
                            ins = nc.tensor.matmul(bank[:, 5 + t // 2, (t % 2) * D:(t % 2 + 1) * D],
                                                   xt[:, a, half, t * P:(t + 1) * P], w_out[:, c, half, :],
                                                   start=(half == n == t % 2 == 0), stop=(half == 1 and n == 2),
                                                   skip_group_check=True)
                        if half == 1 and t % 2:
                            ins.then_inc(s_op, 1)

                def scores_by_key(tau, y):
                    g = tau * NJ + y
                    o = [3 + (g + a) % 4 for a in range(2)]
                    if g >= 4:
                        pe.wait_ge(s_e, b * (NT * NJ) + (g - 2))
                    if y == 0:
                        wait_read(("shift", tau))
                    if g == 0:
                        pe.wait_ge(s_qk, b * 8 + 8)
                        pe.wait_ge(s_vs, b * (2 * T) + T + T)
                    for a in range(2):
                        masks(o[a], diagonals(KEY_JOBS[y + a], True), True)
                    for i in range(len(KEY_JOBS[y])):
                        for a in range(2):
                            _, kb, c = KEY_JOBS[y + a][i]
                            rows = slice(64 * a, 64 * a + 64)
                            ins = nc.tensor.matmul(bank[:, o[a], c:c + L - kb * P],
                                                   stack[rows, tau % 3, 0, kb * P:(kb + 1) * P],
                                                   stack[rows, tau % 3, 1, kb * P:L], start=False, stop=True,
                                                   skip_group_check=True)
                            if i == len(KEY_JOBS[y]) - 1:
                                ins.then_inc(s_k, 1)

                def products_b(tau, y):
                    r, o = tau // 2, 7
                    if tau % 2 == 0 and r >= 1 and y == 0:
                        pe.wait_ge(s_u, b * 4 + r)
                    if tau == 0 and y == 0:
                        pe.wait_ge(s_one, b * 2 + 2)
                    pe.wait_ge(s_e, b * (NT * NJ) + (tau * NJ + y + 2))
                    for i in range(len(KEY_JOBS[y])):
                        for a in range(2):
                            _, kb, c = KEY_JOBS[y + a][i]
                            row = 64 * (tau % 2) + 32 * a
                            at, c0, _ = slot(y + a)
                            ins = nc.tensor.matmul(bank[row:row + 32, o, kb * P:L], vp[:, kb, tau, 2 * a:2 * a + 2, :],
                                                   probs[:, at, c0 + c:c0 + c + L - kb * P], start=(kb == 0),
                                                   stop=(kb == 2), skip_group_check=True, tile_position=(0, row))
                            if i == len(KEY_JOBS[y]) - 1:
                                ins.then_inc(s_pvb, 1)

                def after_scores(tau, n):
                    if n == 0 and 0 <= tau < NT:
                        scores_by_key(tau, 4)
                        products_b(tau, 0)
                    if n == 2 and 0 <= tau < NT:
                        products_b(tau, 2)
                    if n == 2 and tau == -2:
                        for op in range(2):
                            qk_projected(1, op)

                for op in range(2):
                    qk_projected(0, op)
                v_projected(0)
                for tau in range(-3, NT + 1):
                    for job in RING[tau]:
                        if job[0] == "shift":
                            turned_shifts(job[1])
                        elif job[0] == "scores":
                            if job[2] % 2 == 0:
                                scores_by_query(job[1], job[2])
                                after_scores(tau, job[2])
                        elif job[0] == "stack":
                            stacked(job[1], job[2])
                        elif job[0] == "half":
                            turned_half(job[1])
                        else:
                            turned_outputs(job[1])
                    if NT - 2 <= tau < NT:
                        after_scores(tau, 0)
                        after_scores(tau, 2)
                    if 0 <= tau + 1 < NT:
                        scores_by_key(tau + 1, 0)
                        scores_by_key(tau + 1, 2)
                    if 0 <= tau < NT:
                        products_b(tau, 4)
                    if tau == -3:
                        v_projected(1)
                    if tau == NT - 1:
                        output_projected(0)
                output_projected(1)
                ffn(1)


def _layout(n):
    def tiled(a):
        return np.tile(a, P // DK)

    wide = {k: np.asarray(a) for k, a in n.items()}
    none = np.zeros((LEAD, D), np.float32)
    gate = np.concatenate([wide["L0_ffn_gate_w"], none[E:], wide["L0_ffn_shared_gate"],
                           wide["L0_ffn_expert_gate"].reshape(E * I, D)])
    up = np.concatenate([none, wide["L0_ffn_shared_up"], wide["L0_ffn_expert_up"].reshape(E * I, D)])
    down = np.concatenate([none, wide["L0_ffn_shared_down"].T,
                           wide["L0_ffn_expert_down"].transpose(0, 2, 1).reshape(E * I, D)])
    qkv_b = wide["L0_attn_b_qkv_b"]
    maps = [wide[f"L0_attn_a_{k}_w"] for k in ("fq1", "fq2", "fk1", "fk2")]
    vecs = [tiled(wide[f"L0_attn_a_{k}"]) for k in ("fq1_b", "fq2_b", "fk1_b", "fk2_b", "norm_w")]
    vecs += [qkv_b[i * P:(i + 1) * P] for i in range(4)]
    rows = np.stack([qkv_b[2 * D:3 * D], wide["L0_attn_b_out_b"]])
    return {
        "x": wide["L0_attn_a_x"],
        "wqk": np.stack([wide["L0_attn_a_wq"], wide["L0_attn_a_wk"]]),
        "wv_t": wide["L0_attn_a_wv"].T,
        "wo_t": wide["L0_attn_a_wo"].T,
        "fmap": np.stack([np.tile(m.T, (P // DK, 1)) for m in maps], axis=1),
        "vecs": np.stack(vecs, axis=1),
        "qkv_t": wide["L0_attn_b_qkv_w"].T,
        "out_t": wide["L0_attn_b_out_w"].T,
        "rows_b": np.broadcast_to(rows, (P, 2, D)),
        "gu_t": np.stack([gate.T, up.T], axis=1),
        "down_t": down,
        "consts": _constants(),
        "sel": _selector(),
    }


def _constants():
    r = np.arange(P)
    c = np.zeros((P, C_END), np.float32)
    c[:, C_ID:C_ID + P] = r[:, None] == r[None, :]
    c[:, C_TRI:C_TRI + P] = r[:, None] <= r[None, :]
    c[:, C_BD:C_BD + P] = r[:, None] // DK == r[None, :] // DK
    c[:, C_EVEN] = r // DK % 2 == 0
    c[:, C_ODD] = r // DK % 2 == 1
    c[:, C_IOTA:C_IOTA + E] = np.arange(E)
    c[:, C_HALF:C_HALF + H] = -0.5
    c[:, C_ONE] = (r % 64 == SHIFT) | (r % 64 == SHIFT + 1)
    for odd in range(2):
        at = c[:, C_DIAG + odd * DK:C_DIAG + (odd + 1) * DK]
        at[:] = (r[:, None] % DK == np.arange(DK)[None, :]) & (r[:, None] // DK % 2 == odd)
    freqs = np.arange(0, DK, 2, dtype=np.float32) / np.float32(DK)
    angles = np.arange(L, dtype=np.float32)[:, None] * freqs[None, :]
    emb = np.concatenate([np.sin(angles), np.cos(angles)], axis=-1)
    c[:, C_EMB:C_EMB + L] = np.tile(emb.T, (P // DK, 1))
    return c


def _selector():
    s = np.zeros((32, FP - SHARED), np.float32)
    for j in range(E * I):
        s[j // I:3 * E:E, j] = 1.0
    return s


def kernel(**inputs):
    import concourse.bacc as bacc
    from concourse.bass_utils import run_bass_kernel_spmd

    nc = bacc.Bacc("TRN2", target_bir_lowering=False, num_devices=1)
    arrays, args = {}, []
    for name, a in _layout(inputs).items():
        a = np.ascontiguousarray(a)
        arrays[f"in_{name}"] = a
        args.append(nc.dram_tensor(f"in_{name}", a.shape, mybir.dt.from_np(a.dtype), kind="ExternalInput").ap())
    args.append(nc.dram_tensor("out_0", (B, L, D), F32, kind="ExternalOutput").ap())
    build(nc, *args)
    r = run_bass_kernel_spmd(nc, [arrays], core_ids=[0])
    return r.results[0]["out_0"]
```
